# Optimizing a Trainium2 kernel written in Bass

```python
import numpy as np
import jax
import jax.numpy as jnp

def _softmax(x, axis=-1):
    return jax.nn.softmax(x, axis=axis)
def _gelu(x):
    return jax.nn.gelu(x, approximate=True)
def _silu(x):
    return jax.nn.silu(x)
def _sigmoid(x):
    return jax.nn.sigmoid(x)
def _layernorm(x, axis=-1, eps=1e-5):
    m = jnp.mean(x, axis=axis, keepdims=True)
    v = jnp.var(x, axis=axis, keepdims=True)
    return (x - m) / jnp.sqrt(v + eps)
def _scatter_add(tgt, idx, src, axis=0):
    return tgt.at[idx].add(src)
def _segment_sum(src, seg, n):
    return jax.ops.segment_sum(src, seg, n)

kernel_name = 'mk_adj_resnorm_d2_adj_256_128d64'

def setup_inputs(seed: int = 0):
    np.random.seed(seed)
    _w = jnp.asarray
    def _rec_inputs():
        import jax
        import jax.numpy as jnp
        _gk = jax.random.key(seed)
        x = -0.0005207 + 1.001 * jax.random.normal(jax.random.fold_in(_gk, 1), (8, 2048, 256), jnp.float32)
        _a = jax.random.bernoulli(jax.random.fold_in(_gk, 2), 0.015625, (2048, 2048))
        adj = _a.astype(jnp.int32)
        return x, adj
    x, adj = _rec_inputs()
    def _L0_gnn_setup():
        import jax, jax.numpy as jnp
        import numpy as np
        import math
        CHUNK = 256
        NUM_HEADS = 4
        EPS = 1e-05
        key = jax.random.key(seed)
        ks = jax.random.split(key, 12)
        B, N, F = (4, 2048, 256)
        x = jax.random.normal(ks[0], (B, N, F), dtype=jnp.float32)
        adj_matrix = jax.random.randint(ks[1], (N, N), 0, 2, dtype=jnp.int32)
        s = 1.0 / math.sqrt(F)
        Wq = jax.random.normal(ks[2], (F, F), dtype=jnp.float32) * s
        bq = jnp.zeros((F,), dtype=jnp.float32)
        Wk = jax.random.normal(ks[3], (F, F), dtype=jnp.float32) * s
        bk = jnp.zeros((F,), dtype=jnp.float32)
        Wv = jax.random.normal(ks[4], (F, F), dtype=jnp.float32) * s
        bv = jnp.zeros((F,), dtype=jnp.float32)
        Wo = jax.random.normal(ks[5], (F, F), dtype=jnp.float32) * s
        bo = jnp.zeros((F,), dtype=jnp.float32)
        gamma = jnp.ones((F,), dtype=jnp.float32)
        beta = jnp.zeros((F,), dtype=jnp.float32)
        return {'x': x, 'adj_matrix': adj_matrix, 'Wq': Wq, 'bq': bq, 'Wk': Wk, 'bk': bk, 'Wv': Wv, 'bv': bv, 'Wo': Wo, 'bo': bo, 'gamma': gamma, 'beta': beta}
    _L0_gnn_all = _L0_gnn_setup()
    _L0_gnn_in = {k: v for k, v in _L0_gnn_all.items() if k in ('Wq', 'bq', 'Wk', 'bk', 'Wv', 'bv', 'Wo', 'bo', 'gamma', 'beta', )}
    del _L0_gnn_all

    def _L1_gnn_setup():
        import jax, jax.numpy as jnp
        import numpy as np
        B, N, IN_F = (8, 1024, 256)
        N_H, D_F = (4, 64)
        NEG_SLOPE = 0.2
        key = jax.random.key(seed)
        k1, k2, k3, k4 = jax.random.split(key, 4)
        h = jax.random.normal(k1, (B, N, IN_F), dtype=jnp.float32)
        adj = jax.random.randint(k2, (N, N), 0, 2, dtype=jnp.int32)
        W = jax.random.normal(k3, (IN_F, N_H * D_F), dtype=jnp.float32) * IN_F ** (-0.5)
        a = jax.random.normal(k4, (N_H, 2 * D_F), dtype=jnp.float32) * D_F ** (-0.5)
        return {'h': h, 'adj': adj, 'W': W, 'a': a}
    _L1_gnn_all = _L1_gnn_setup()
    _L1_gnn_in = {k: v for k, v in _L1_gnn_all.items() if k in ('W', 'a', )}
    del _L1_gnn_all

    return {
        "x": x,
        "adj": adj,
        "L0_gnn_Wq": _L0_gnn_in["Wq"],
        "L0_gnn_bq": _L0_gnn_in["bq"],
        "L0_gnn_Wk": _L0_gnn_in["Wk"],
        "L0_gnn_bk": _L0_gnn_in["bk"],
        "L0_gnn_Wv": _L0_gnn_in["Wv"],
        "L0_gnn_bv": _L0_gnn_in["bv"],
        "L0_gnn_Wo": _L0_gnn_in["Wo"],
        "L0_gnn_bo": _L0_gnn_in["bo"],
        "L0_gnn_gamma": _L0_gnn_in["gamma"],
        "L0_gnn_beta": _L0_gnn_in["beta"],
        "L1_gnn_W": _L1_gnn_in["W"],
        "L1_gnn_a": _L1_gnn_in["a"],
    }

def reference(x, adj, L0_gnn_Wq, L0_gnn_bq, L0_gnn_Wk, L0_gnn_bk, L0_gnn_Wv, L0_gnn_bv, L0_gnn_Wo, L0_gnn_bo, L0_gnn_gamma, L0_gnn_beta, L1_gnn_W, L1_gnn_a):
    import jax
    import jax.numpy as jnp
    def _L0_gnn_ref(x, adj_matrix, Wq, bq, Wk, bk, Wv, bv, Wo, bo, gamma, beta):
        import jax, jax.numpy as jnp
        import numpy as np
        import math
        CHUNK = 256
        NUM_HEADS = 4
        EPS = 1e-05
        B, N, Fin = x.shape
        H = NUM_HEADS
        Dout = Wq.shape[0]
        Dh = Dout // H
        Nc = N // CHUNK
        q = (x @ Wq.T + bq).reshape(B, N, H, Dh).transpose(0, 2, 1, 3)
        k = (x @ Wk.T + bk).reshape(B, N, H, Dh).transpose(0, 2, 1, 3)
        v = (x @ Wv.T + bv).reshape(B, N, H, Dh).transpose(0, 2, 1, 3)
        kc = k.reshape(B, H, Nc, CHUNK, Dh)
        vc = v.reshape(B, H, Nc, CHUNK, Dh)
        scores = jnp.einsum('bhnd,bhjcd->bhnjc', q, kc) / jnp.sqrt(jnp.asarray(Dh, dtype=q.dtype))
        scores = jnp.clip(scores, -10.0, 10.0)
        mask = adj_matrix.reshape(N, Nc, CHUNK)[None, None]
        scores = jnp.where(mask == 0, jnp.asarray(-10.0, scores.dtype), scores)
        attn = jax.nn.softmax(scores, axis=-1)
        ctx = jnp.einsum('bhnjc,bhjcd->bhnd', attn, vc)
        ctx = ctx.transpose(0, 2, 1, 3).reshape(B, N, Dout)
        out = ctx @ Wo.T + bo
        out = out + x
        mu = jnp.mean(out, axis=-1, keepdims=True)
        var = jnp.mean(jnp.square(out - mu), axis=-1, keepdims=True)
        out = (out - mu) * jax.lax.rsqrt(var + EPS) * gamma + beta
        return out

    def _L1_gnn_ref(h, adj, W, a):
        import jax, jax.numpy as jnp
        import numpy as np
        B, N, IN_F = (8, 1024, 256)
        N_H, D_F = (4, 64)
        NEG_SLOPE = 0.2
        Wh = (h @ W).reshape(h.shape[0], h.shape[1], N_H, D_F)
        a_src, a_dst = (a[:, :D_F], a[:, D_F:])
        s_src = jnp.einsum('bnhd,hd->bnh', Wh, a_src)
        s_dst = jnp.einsum('bnhd,hd->bnh', Wh, a_dst)
        e = s_src[:, :, None, :] + s_dst[:, None, :, :]
        e = jnp.where(e > 0, e, NEG_SLOPE * e)
        mask = (adj != 0)[None, :, :, None]
        e = jnp.where(mask, e, -jnp.inf)
        alpha = jax.nn.softmax(e, axis=2)
        alpha = jnp.nan_to_num(alpha, nan=0.0)
        h_out = jnp.einsum('bijh,bjhd->bihd', alpha, Wh)
        h_out = h_out.reshape(h.shape[0], h.shape[1], N_H * D_F)
        return jax.nn.elu(h_out)

    x = _layernorm(x + _L0_gnn_ref(x, adj, L0_gnn_Wq, L0_gnn_bq, L0_gnn_Wk, L0_gnn_bk, L0_gnn_Wv, L0_gnn_bv, L0_gnn_Wo, L0_gnn_bo, L0_gnn_gamma, L0_gnn_beta), axis=-1)
    x = _layernorm(x + _L1_gnn_ref(x, adj, L1_gnn_W, L1_gnn_a), axis=-1)
    return x


_drawn_inputs = setup_inputs


def setup_inputs(seed=0):
    import zlib

    import numpy as np

    out = dict(_drawn_inputs(seed))
    spreads = {'L0_gnn_bq': (0.0, 0.269),
     'L0_gnn_bk': (0.0, 2.0),
     'L0_gnn_bv': (0.0, 0.1),
     'L0_gnn_bo': (0.0, 0.1),
     'L0_gnn_gamma': (1.0, 0.2),
     'L0_gnn_beta': (0.0, 0.1)}
    factors = {}
    for name, (base, spread) in spreads.items():
        noise = np.random.default_rng([zlib.crc32(name.encode()), seed]).standard_normal(out[name].shape)
        drawn = base * np.exp(spread * noise) if base else spread * noise
        out[name] = jnp.asarray(drawn.astype(out[name].dtype))
    for name, factor in factors.items():
        out[name] = (out[name] * factor).astype(out[name].dtype)
    return out
```

```python
from contextlib import ExitStack

import concourse.bass as bass
from concourse import mybir

ALU = mybir.AluOpType
ACT = mybir.ActivationFunctionType
AX = mybir.AxisListType
F32 = mybir.dt.float32
F16 = mybir.dt.float16
BF16 = mybir.dt.bfloat16
I32 = mybir.dt.int32
I8 = mybir.dt.int8

P = 128
B, N, F = 8, 2048, 256
H, D = 4, 64
CHUNK = 256
NC = N // CHUNK
NT = N // P
NG = N // 512
FT = F // P
DV = D + 1
CLIP = 80.0
EPS = 1e-5
SHIFT = 40.0
R_MAX = 1e30
UNITS0 = H * NG
UNITS1 = H * NT
SLOTS = 7


def build(nc, x, adj, Wq, bq, Wk, bk, Wv, bv, Wo, bo, gamma, beta, W1, a1, out):
    with ExitStack() as ctx:
        def sb(name, shape, dt):
            return ctx.enter_context(nc.sbuf_tensor(name, shape, dt))

        def sem(name):
            return ctx.enter_context(nc.semaphore(name))

        clip_hi = sb("clip_hi", [P, NT, N], I8)
        edge = sb("edge", [P, NT * N], I8)
        x_keep = sb("x_keep", [P, NT, F], F32)
        reg_t = sb("reg_t", [P, 4096], F32)
        reg_c = sb("reg_c", [P, 4096], F32)
        reg_q = sb("reg_q", [P, 8192], F32)
        reg_k = sb("reg_k", [P, 4096], F32)
        v1 = sb("v1", [P, NC * H * 2 * DV], F32)
        nz = sb("nz", [P, 2, N], BF16)
        w_t = sb("w_t", [P, 4, FT, F], F32)
        w1 = sb("w1", [P, FT, F], F32)
        wa = sb("wa", [P, 2, FT, H], F32)
        b_qk = sb("b_qk", [P, 2, FT], F32)
        bv_all = sb("bv_all", [P, F], F32)
        gamma_all = sb("gamma_all", [P, F], F32)
        beta_all = sb("beta_all", [P, F], F32)
        bo_row = sb("bo_row", [1, 2, F], F32)
        bo_less_beta = sb("bo_less_beta", [1, F], F32)
        ident = sb("ident", [P, P], F32)
        ident_b = sb("ident_b", [P, P], BF16)
        ones = sb("ones", [4, P], F32)
        consts = sb("consts", [P, 2], F32)
        scaled = sb("scaled", [P, 4, 4, D], F32)
        rden = sb("rden", [P, 4, 4], F32)
        stats = sb("stats", [P, NT, 6], F32)
        mv = sb("mv", [P, NT, 2], F32)
        std = sb("std", [P, NT], F32)
        rstd = sb("rstd", [P, NT], F32)
        gat_max = sb("gat_max", [P, H], F32)
        gat_max4 = sb("gat_max4", [H, 1], F32)
        gat_rbias = sb("gat_rbias", [H, 1], F32)
        gat_diag = sb("gat_diag", [H, H], F32)
        gat_b = sb("gat_b", [P, H], F32)
        gat_d = sb("gat_d", [P, H, NT], F32)
        gat_x = sb("gat_x", [P, H, NT], F32)
        gat_nx = sb("gat_nx", [P, H, NT], F32)
        gat_y = sb("gat_y", [P, H, NT], F32)
        gat_den = sb("gat_den", [P, 3 * SLOTS], F32)
        gat_rden = sb("gat_rden", [P, 3 * SLOTS], F32)

        x_t = reg_t[:, :].rearrange("p (f n) -> p f n", f=FT)
        clipped_s = reg_t[:, 0:2048].rearrange("p (u j n) -> p u j n", u=2, j=2)
        probs0 = reg_t[:, 2048:4096].rearrange("p (u j n) -> p u j n", u=2, j=2)
        r_row = reg_t[0:H, 0:N]
        ctxs = reg_c[:, :].rearrange("p (t f) -> p t f", f=F)
        parts = reg_c[:, :].bitcast(F16).rearrange("p (k n) -> p k n", k=4)
        w_nat = reg_c[:, 0:4 * FT * F].rearrange("p (w t f) -> p w t f", w=4, t=FT)
        a_all = reg_c[:, 2048:2048 + 2 * H * D].rearrange("p (h s d) -> p h s d", h=H, s=2)
        wa_prod = reg_c[:, 2560:2560 + FT * 2 * H * D].rearrange("p (t s h d) -> p t s h d", t=FT, s=2, h=H)
        q16 = reg_q[:, :].bitcast(F16).rearrange("p (k h n) -> p k h n", k=2, h=H)
        relu1 = reg_q[:, 0:4096].rearrange("p (u n) -> p u n", u=2)
        probs1 = reg_q[:, 4096:8192].rearrange("p (u n) -> p u n", u=2)
        elu_e = reg_q[:, 0:4096].rearrange("p (t f) -> p t f", f=F)
        k16 = reg_k[:, :].bitcast(F16)
        k16_v = k16.rearrange("p (c h n) -> p c h n", c=NC, h=H)
        r_all = reg_k[:, :].rearrange("p (u n) -> p u n", u=2)
        adj_rows = reg_k[:, :].bitcast(I32).rearrange("p (u n) -> p u n", u=2)
        v1_v = v1[:, :].rearrange("p (c h t d) -> p c h t d", c=NC, h=H, t=2)

        ps = ctx.enter_context(nc.psum_tensor("ps", [P, 8, 512], F32))

        r_dram = nc.dram_tensor("r_scratch", (B, H, N), F32, kind="Internal").ap()

        s_w = sem("weights_loaded")
        s_adj = [sem(f"adj_loaded{i}") for i in range(2)]
        s_const = sem("consts_set")
        s_ones = sem("ones_set")
        s_setup = sem("setup_small")
        s_nz = sem("nz_made")
        s_adj_t = sem("adj_turned")
        s_clipm = sem("clip_hi_made")
        s_edge = sem("edge_made")
        s_wturn = sem("weights_turned")
        s_wcopy = sem("weights_copied")
        s_x = [sem(f"x_loaded{g}") for g in range(NG)]
        s_turn = sem("turn_filled")
        s_turn_a = sem("turn_copied_scalar")
        s_turn_v = sem("turn_copied_vector")
        s_qk = sem("qk_filled")
        s_hi = sem("hi_made")
        s_lo = sem("lo_made")
        s_v = sem("v_filled")
        s_vc = sem("v_copied")
        s_beta = sem("beta_added")
        s_stack = [sem(f"heads_stacked{i}") for i in range(FT)]
        s_s0 = sem("scores0_filled")
        s_cl = sem("scores0_clipped")
        s_e0 = sem("probs0_made")
        s_o0 = sem("ctx0_filled")
        s_rd = sem("rden_made")
        s_sc = sem("ctx0_scaled")
        s_add = sem("ctx0_added")
        s_zero = sem("ctx0_zeroed")
        s_wo = sem("wo_filled")
        s_r = sem("resid_made")
        s_st = sem("ln_stats")
        s_ag = sem("ln_aggregated")
        s_sq = sem("ln_std")
        s_rs = sem("ln_rstd")
        s_z = sem("ln_steps")
        s_x1 = sem("x1_made")
        s_wh = sem("wh_filled")
        s_whc = sem("wh_copied")
        s_sd = sem("gat_filled")
        s_gv = sem("gat_vector")
        s_xy = sem("gat_scalar")
        s_rr = sem("r_row_made")
        s_rs_dma = sem("r_row_stored")
        s_rl = [sem(f"r_loaded{i}") for i in range(2)]
        s_re = sem("relu1_made")
        s_m1 = sem("probs1_made")
        s_o1 = sem("ctx1_filled")
        s_d1 = sem("den1_steps")
        s_c1 = sem("ctx1_scaled")
        s_x1m = sem("x1_less_one")
        s_ee = sem("elu_exp_made")
        s_y = sem("elu_steps")
        s_res = sem("result_made")
        s_out = sem("out_stored")

        s_gate_p = sem("pool_went_on")
        s_gate_v = sem("vector_went_on")

        block = ctx.enter_context(nc.Block())

        @block.sync
        def _(sp):
            for s, n in ((s_cl, 2), (s_e0, 2), (s_o0, 2), (s_sc, 4), (s_add, 4), (s_m1, 2), (s_o1, 2),
                         (s_c1, 2), (s_re, 2), (s_res, 1), (s_out, 16)):
                sp.sem_inc(s, n)
            for k, w in enumerate((Wq, Wk, Wv, Wo)):
                sp.dma_start(w_nat[:, k, :, :], w.rearrange("(t p) f -> p t f", p=P)).then_inc(s_w, 16)
            sp.dma_start(w1[:, :, :], W1.rearrange("(t p) f -> p t f", p=P)).then_inc(s_w, 16)
            sp.dma_start(a_all, a1.rearrange("h (s d) -> h s d", s=2).partition_broadcast(P)).then_inc(s_w, 16)
            for k, v in enumerate((bq, bk)):
                sp.dma_start(b_qk[:, k, :], v.rearrange("(t p) -> p t", p=P),
                             allow_slow_non_contiguous=True).then_inc(s_w, 16)
            for t, v in ((bv_all, bv), (gamma_all, gamma), (beta_all, beta)):
                sp.dma_start(t[:, :], v.partition_broadcast(P)).then_inc(s_w, 16)
            for k, v in enumerate((bo, beta)):
                sp.dma_start(bo_row[0:1, k, :], v.partition_broadcast(1)).then_inc(s_w, 16)
            for t in range(NT):
                if t >= 2:
                    sp.wait_ge(s_nz, t - 1)
                sp.dma_start(adj_rows[:, t % 2, :], adj[t * P:(t + 1) * P, :]).then_inc(s_adj[t % 2], 16)
            with sp.Fori(0, B) as b:
                sp.wait_ge(s_res, b * NG + 1)
                xb = x[bass.ds(b, 1), :, :].rearrange("o (t p) f -> p (o t) f", p=P)
                for g in range(NG):
                    sp.dma_start(x_keep[:, 4 * g:4 * g + 4, :], xb[:, 4 * g:4 * g + 4, :]).then_inc(s_x[g], 16)
                for p in range(FT):
                    sp.wait_ge(s_hi, b * 16 + 8 * (p + 1))
                    sp.wait_ge(s_lo, b * 16 + 8 * (p + 1))
                    for e in range(2):
                        h, rows = 2 * p + e, slice(D * e, D * e + D)
                        for k in range(2):
                            for half in (slice(0, D), slice(D, P)):
                                sp.dma_start(q16[half, k, h, :], parts[rows, k, :]).then_inc(s_stack[p], 16)
                            half = slice(D * k, D * k + D)
                            sp.dma_start(k16_v[half, :, h, :], parts[rows, 2 + k, :].rearrange(
                                "p (c n) -> p c n", c=NC)).then_inc(s_stack[p], 16)
                sp.wait_ge(s_rr, b + 1)
                rb = r_dram[bass.ds(b, 1), :, :]
                sp.dma_start(rb.rearrange("o h n -> (o h) n"), r_row).then_inc(s_rs_dma, 16)
                sp.wait_ge(s_rs_dma, 16 * b + 16)
                for h in range(H):
                    if h >= 2:
                        sp.wait_ge(s_re, b * UNITS1 + (h - 1) * NT + 2)
                    row = rb[:, h, :].rearrange("o n -> (o n)").partition_broadcast(P)
                    sp.dma_start(r_all[:, h % 2, :], row).then_inc(s_rl[h % 2], 16)
                ob = out[bass.ds(b, 1), :, :].rearrange("o (t p) f -> p (o t) f", p=P)
                for g in range(NG):
                    sp.wait_ge(s_res, b * NG + g + 2)
                    sp.dma_start(ob[:, 4 * g:4 * g + 4, :], ctxs[:, 4 * g:4 * g + 4, :]).then_inc(s_out, 16)
            sp.wait_ge(s_out, 16 * NG * B + 16)

        @block.gpsimd
        def _(pool):
            nc.gpsimd.memset(ident[:, :], 0.0).then_inc(s_ones, 1)
            nc.gpsimd.memset(ones[:, :], 1.0).then_inc(s_ones, 1)
            nc.gpsimd.memset(consts[:, 0:1], EPS).then_inc(s_ones, 1)
            nc.gpsimd.memset(consts[:, 1:2], SHIFT).then_inc(s_ones, 1)
            nc.gpsimd.memset(v1_v[:, :, :, :, D:DV].rearrange("p c h t d -> p (c h t) d"), 1.0).then_inc(s_ones, 1)
            pool.wait_ge(s_ones, 5)
            nc.gpsimd.affine_select(out=ident[:, :], in_=ident[:, :], compare_op=ALU.not_equal, fill=1.0,
                                    base=0, pattern=[[-1, P]], channel_multiplier=1).then_inc(s_ones, 1)
            pool.wait_ge(s_ones, 6)
            nc.gpsimd.tensor_copy(ident_b[:, :], ident[:, :]).then_inc(s_const, 1)
            pool.wait_ge(s_clipm, 2 * NT)
            for j in range(NT):
                nc.gpsimd.tensor_scalar(edge[:, j * N:j * N + N], clip_hi[:, j, :], 0.5 / CLIP, 0.5,
                                        ALU.mult, ALU.add).then_inc(s_edge, 1)
            with pool.Fori(0, B) as b:
                pool.wait_ge(s_turn, b * 24 + 8)
                pool.wait_ge(s_w, 16 * 13)
                nc.gpsimd.tensor_tensor(x_keep[:, :, :], x_keep[:, :, :],
                                        beta_all[:, :].unsqueeze(1).to_broadcast([P, NT, F]),
                                        ALU.add).then_inc(s_beta, 1)
                for p in range(FT):
                    pool.wait_ge(s_stack[p], (b + 1) * 192)
                pool.sem_inc(s_gate_p, 1)
                nc.gpsimd.memset(reg_c[:, :], 0.0).then_inc(s_zero, 1)
                pool.wait_ge(s_zero, b + 1)
                pool.sem_inc(s_gate_p, 1)
                with pool.Fori(0, NC) as c:
                    for n in range(UNITS0):
                        h, g = n // NG, n % NG
                        pool.wait_ge(s_sc, b * (NC * UNITS0) + c * UNITS0 + n + 5)
                        acc = ctxs[:, 4 * g:4 * g + 4, h * D:h * D + D]
                        nc.gpsimd.tensor_tensor(acc, acc, scaled[:, n % 4, :, :], ALU.add).then_inc(s_add, 1)
                pool.wait_ge(s_turn, b * 24 + 24)
                pool.sem_inc(s_gate_p, 1)
                nc.gpsimd.tensor_scalar(x_keep[:, :, :], x_keep[:, :, :], 1.0, -1.0,
                                        ALU.mult, ALU.add).then_inc(s_x1m, 1)

        @block.tensor
        def _(pe):
            pe.wait_ge(s_const, 1)
            pe.wait_ge(s_w, 16 * 13)
            for k in range(4):
                for f in range(FT):
                    m = k * FT + f
                    if m >= 4:
                        pe.wait_ge(s_wcopy, m - 3)
                    for t in range(FT):
                        last = nc.tensor.transpose(ps[:, m % 4, t * P:t * P + P],
                                                   w_nat[:, k, t, f * P:f * P + P], ident[:, :])
                    last.then_inc(s_wturn, 1)
            pe.wait_ge(s_wcopy, 4 * FT)
            for t in range(NT):
                pe.wait_ge(s_nz, t + 1)
                for half in range(2):
                    m = 2 * t + half
                    if m >= 4:
                        pe.wait_ge(s_clipm, m - 3)
                    bank = ps[:, m % 4, :].bitcast(BF16)
                    for j in range(8):
                        jt = 8 * half + j
                        last = nc.tensor.transpose(bank[:, j * P:j * P + P],
                                                   nz[:, t % 2, jt * P:jt * P + P], ident_b[:, :])
                    last.then_inc(s_adj_t, 1)
            pe.wait_ge(s_clipm, 2 * NT)

            def turn(b, r, src, ready):
                for m in range(2 * NG):
                    g, f = m // 2, m % 2
                    if f == 0:
                        ready(g)
                    if m >= 4:
                        pe.wait_ge(s_turn_v if f else s_turn_a, b * 12 + 4 * r + (m - 4) // 2 + 1)
                    for t in range(4):
                        last = nc.tensor.transpose(ps[:, m % 4, t * P:t * P + P],
                                                   src[:, 4 * g + t, f * P:f * P + P], ident[:, :])
                    last.then_inc(s_turn, 1)

            def turned(b, r):
                pe.wait_ge(s_turn_a, b * 12 + 4 * r + 4)
                pe.wait_ge(s_turn_v, b * 12 + 4 * r + 4)

            def tokens_by_features(m, w, row=None):
                for t in range(2):
                    o = ps[:, m % 4, t * F:t * F + F]
                    tok = slice((2 * m + t) * P, (2 * m + t + 1) * P)
                    for f in range(FT):
                        last = nc.tensor.matmul(o, x_t[:, f, tok], w[:, f, :], start=(f == 0),
                                                stop=(f == FT - 1 and row is None))
                    if row is not None:
                        last = nc.tensor.matmul(o, ones[0:1, :], row, start=False, stop=True)
                return last

            def project_qk(b, p):
                for m in range(2 * NG):
                    g, k = m // 2, m % 2
                    if m >= 4:
                        pe.wait_ge(s_lo, b * 16 + 8 * p + m - 3)
                    for f in range(FT):
                        last = nc.tensor.matmul(ps[:, m % 4, :], w_t[:, k, f, p * P:p * P + P],
                                                x_t[:, f, g * 512:g * 512 + 512],
                                                start=(f == 0), stop=(f == FT - 1))
                    last.then_inc(s_qk, 1)

            def scores0(b, c, n):
                h, g = n // NG, n % NG
                pe.wait_ge(s_cl, b * (NC * UNITS0) + c * UNITS0 + n + 1)
                for j in range(2):
                    o = ps[:, 2 * (n % 2) + j, :]
                    keys = k16[:, bass.ds(c * (H * CHUNK) + h * CHUNK + j * P, P)]
                    for k in range(2):
                        last = nc.tensor.matmul(o, keys, q16[:, k, h, g * 512:g * 512 + 512],
                                                start=(k == 0), stop=(k == 1))
                last.then_inc(s_s0, 1)

            def context0(b, c, n):
                h = n // NG
                unit = b * (NC * UNITS0) + c * UNITS0 + n
                pe.wait_ge(s_e0, unit + 3)
                pe.wait_ge(s_sc, unit + 1)
                for j in range(2):
                    for t in range(4):
                        last = nc.tensor.matmul(
                            ps[:, 4 + n % 4, t * DV:t * DV + DV], probs0[:, n % 2, j, t * P:t * P + P],
                            v1[:, bass.ds(c * (2 * H * DV) + (2 * h + j) * DV, DV)],
                            start=(j == 0 and t == 0), stop=(j == 1), skip_group_check=True)
                last.then_inc(s_o0, 1)

            def chunk0(b, c, first):
                for n in range(UNITS0):
                    scores0(b, c, n)
                    if n >= 2:
                        context0(b, c, n - 2)
                    elif not first:
                        context0(b, c - 1, n - 2 + UNITS0)

            def context1(b, h, jj, k, first):
                unit = b * UNITS1 + h * NT + 2 * jj + k
                pe.wait_ge(s_m1, unit + 3)
                for t in range(NT):
                    bank, slot = 4 * (h % 2) + t // SLOTS, t % SLOTS
                    last = nc.tensor.matmul(
                        ps[:, bank, slot * DV:slot * DV + DV], probs1[:, k, t * P:t * P + P],
                        v1[:, bass.ds(jj * (2 * H * DV) + (2 * h + k) * DV, DV)],
                        start=(first and slot == 0), stop=False, skip_group_check=True)
                last.then_inc(s_o1, 1)

            with pe.Fori(0, B) as b:
                pe.wait_ge(s_c1, b * H + 2)
                turn(b, 0, x_keep, lambda g: pe.wait_ge(s_x[g], 16 * b + 16))
                turned(b, 0)
                project_qk(b, 0)
                pe.wait_ge(s_lo, b * 16 + 8)
                for m in range(NC):
                    if m >= 4:
                        pe.wait_ge(s_vc, b * NC + m - 3)
                    tokens_by_features(m, w_t[:, 2, :, :]).then_inc(s_v, 1)
                pe.wait_ge(s_vc, b * NC + NC)
                project_qk(b, 1)
                pe.wait_ge(s_lo, b * 16 + 16)
                pe.wait_ge(s_stack[0], (b + 1) * 192)
                pe.wait_ge(s_stack[1], (b + 1) * 192)
                chunk0(b, 0, True)
                with pe.Fori(1, NC) as c:
                    chunk0(b, c, False)
                context0(b, NC - 1, UNITS0 - 2)
                context0(b, NC - 1, UNITS0 - 1)
                turn(b, 1, ctxs, lambda g: pe.wait_ge(s_add, (b + 1) * (NC * UNITS0) + 4) if g == 0 else None)
                turned(b, 1)
                for m in range(NC):
                    if m >= 4:
                        pe.wait_ge(s_r, b * NC + m - 3)
                    tokens_by_features(m, w_t[:, 3, :, :], bo_less_beta[0:1, :]).then_inc(s_wo, 1)
                turn(b, 2, x_keep, lambda g: pe.wait_ge(s_x1, b * NG + g + 1))
                turned(b, 2)
                for t in range(NT):
                    for f in range(FT):
                        last = nc.tensor.matmul(ps[:, 7, t * H:t * H + H], x_t[:, f, t * P:t * P + P],
                                                wa[:, 1, f, :], start=(f == 0), stop=(f == FT - 1))
                last.then_inc(s_sd, 1)
                for m in range(NC):
                    if m >= 4:
                        pe.wait_ge(s_whc, b * NC + m - 3)
                    tokens_by_features(m, w1).then_inc(s_wh, 1)
                    if m == 3:
                        pe.wait_ge(s_gv, b * 8 + 1)
                        nc.tensor.transpose(ps[0:H, 6, 0:P], gat_max[:, :], ident[:, :]).then_inc(s_sd, 1)
                    if m == 6:
                        pe.wait_ge(s_gv, b * 8 + 4)
                        nc.tensor.matmul(ps[:, 5, 0:H], ones[0:H, :], gat_diag[:, :],
                                         start=True, stop=True).then_inc(s_sd, 1)
                pe.wait_ge(s_whc, b * NC + NC)
                for g in range(NG):
                    for f in range(FT):
                        last = nc.tensor.matmul(ps[0:H, g, :], wa[:, 0, f, :], x_t[:, f, g * 512:g * 512 + 512],
                                                start=(f == 0), stop=(f == FT - 1))
                last.then_inc(s_sd, 1)
                pe.wait_ge(s_xy, b * 3 + 1)
                for h in range(H):
                    pe.wait_ge(s_c1, b * H + h + 1)
                    context1(b, h, 0, 0, True)
                    context1(b, h, 0, 1, False)
                    with pe.Fori(1, NT // 2) as jj:
                        context1(b, h, jj, 0, False)
                        context1(b, h, jj, 1, False)

        @block.scalar
        def _(act):
            def turn(b, r):
                for g in range(NG):
                    act.wait_ge(s_turn, b * 24 + 8 * r + 2 * g + 1)
                    nc.scalar.activation(x_t[:, 0, g * 512:g * 512 + 512], ps[:, (2 * g) % 4, :],
                                         ACT.Copy).then_inc(s_turn_a, 1)

            def high_parts(b, p):
                for m in range(2 * NG):
                    g, k = m // 2, m % 2
                    act.wait_ge(s_qk, b * 16 + 8 * p + m + 1)
                    nc.scalar.activation(parts[:, 2 * k, g * 512:g * 512 + 512], ps[:, m % 4, :], ACT.Identity,
                                         bias=b_qk[:, k, p:p + 1]).then_inc(s_hi, 1)

            def exp0(b, c, n):
                unit = b * (NC * UNITS0) + c * UNITS0 + n
                act.wait_ge(s_cl, unit + 3)
                act.wait_ge(s_o0, unit + 1)
                nc.scalar.activation(probs0[:, n % 2, :, :], clipped_s[:, n % 2, :, :], ACT.Exp,
                                     scale=0.125).then_inc(s_e0, 1)

            def relu1_unit(b, h, jj, k):
                unit = b * UNITS1 + h * NT + 2 * jj + k
                act.wait_ge(s_m1, unit + 1)
                j = bass.ds(2 * jj + k, 1)
                nc.scalar.activation(relu1[:, k, :], r_all[:, h % 2, :], ACT.Relu,
                                     scale=gat_y[:, h, j], bias=gat_nx[:, h, j]).then_inc(s_re, 1)

            with act.Fori(0, B) as b:
                turn(b, 0)
                act.wait_ge(s_out, 16 * NG * b + 16)
                act.wait_ge(s_w, 16 * 13)
                high_parts(b, 0)
                act.wait_ge(s_stack[0], (b + 1) * 192)
                high_parts(b, 1)
                with act.Fori(0, NC) as c:
                    for n in range(UNITS0):
                        exp0(b, c, n)
                turn(b, 1)
                for r in range(2):
                    act.wait_ge(s_ag, b * 3 + r + 1)
                    nc.scalar.activation(std[:, :], mv[:, :, 1], ACT.Sqrt, bias=consts[:, 0:1]).then_inc(s_sq, 1)
                turn(b, 2)
                for m in range(NC):
                    act.wait_ge(s_wh, b * NC + m + 1)
                    nc.scalar.activation(v1_v[:, m, :, :, 0:D],
                                         ps[:, m % 4, :].rearrange("p (t h d) -> p h t d", t=2, h=H),
                                         ACT.Copy).then_inc(s_whc, 1)
                act.wait_ge(s_gv, b * 8 + 3)
                act.wait_ge(s_sd, b * 4 + 4)
                nc.scalar.activation(r_row.rearrange("h (g n) -> h g n", g=NG), ps[0:H, 0:NG, :], ACT.Exp,
                                     scale=-0.8, bias=gat_rbias[:, :]).then_inc(s_xy, 1)
                act.wait_ge(s_gv, b * 8 + 6)
                nc.scalar.activation(gat_x[:, :, :], gat_d[:, :, :], ACT.Exp, bias=consts[:, 1:2]).then_inc(s_xy, 1)
                nc.scalar.activation(gat_y[:, :, :], gat_d[:, :, :], ACT.Exp, scale=0.2).then_inc(s_xy, 1)
                act.wait_ge(s_xy, b * 3 + 3)
                act.wait_ge(s_gv, b * 8 + 8)
                for h in range(H):
                    act.wait_ge(s_rl[h % 2], 32 * b + 16 * (h // 2) + 16)
                    with act.Fori(0, NT // 2) as jj:
                        relu1_unit(b, h, jj, 0)
                        relu1_unit(b, h, jj, 1)
                for g in range(NG):
                    act.wait_ge(s_c1, b * H + H + 2)
                    nc.scalar.activation(elu_e[:, 4 * g:4 * g + 4, :], ctxs[:, 4 * g:4 * g + 4, :],
                                         ACT.Exp).then_inc(s_ee, 1)
                act.wait_ge(s_ag, b * 3 + 3)
                nc.scalar.activation(std[:, :], mv[:, :, 1], ACT.Sqrt, bias=consts[:, 0:1]).then_inc(s_sq, 1)

        @block.vector
        def _(dve):
            dve.wait_ge(s_w, 16 * 13)
            for f in range(FT):
                for s in range(2):
                    nc.vector.tensor_tensor(wa_prod[:, f, s, :, :], w1[:, f, :].rearrange("p (h d) -> p h d", h=H),
                                            a_all[:, :, s, :], ALU.mult).then_inc(s_setup, 1)
            nc.vector.tensor_tensor(bo_less_beta[:, :], bo_row[:, 0, :], bo_row[:, 1, :],
                                    ALU.subtract).then_inc(s_setup, 1)
            dve.wait_ge(s_setup, 5)
            for f in range(FT):
                for s in range(2):
                    nc.vector.tensor_reduce(wa[:, s, f, :], wa_prod[:, f, s, :, :], AX.X, ALU.add).then_inc(s_setup, 1)
            for m in range(4 * FT):
                dve.wait_ge(s_wturn, m + 1)
                nc.vector.tensor_copy(w_t[:, m // FT, m % FT, :], ps[:, m % 4, 0:F]).then_inc(s_wcopy, 1)
            def marks(t):
                dve.wait_ge(s_adj[t % 2], 16 * (t // 2) + 16)
                if t >= 2:
                    dve.wait_ge(s_adj_t, 2 * (t - 1))
                nc.vector.tensor_scalar(nz[:, t % 2, :], adj_rows[:, t % 2, :], 0.0, None,
                                        ALU.not_equal).then_inc(s_nz, 1)

            marks(0)
            for t in range(NT):
                if t + 1 < NT:
                    marks(t + 1)
                for half in range(2):
                    m = 2 * t + half
                    dve.wait_ge(s_adj_t, m + 1)
                    nc.vector.tensor_scalar(clip_hi[:, 8 * half:8 * half + 8, t * P:t * P + P],
                                            ps[:, m % 4, :].bitcast(BF16).rearrange("p (j n) -> p j n", j=8),
                                            2 * CLIP, -CLIP, ALU.mult, ALU.add).then_inc(s_clipm, 1)
            dve.wait_ge(s_clipm, 2 * NT)

            def turn(b, r):
                for g in range(NG):
                    dve.wait_ge(s_turn, b * 24 + 8 * r + 2 * g + 2)
                    nc.vector.tensor_copy(x_t[:, 1, g * 512:g * 512 + 512],
                                          ps[:, (2 * g + 1) % 4, :]).then_inc(s_turn_v, 1)

            def low_parts(b, p):
                for m in range(2 * NG):
                    g, k = m // 2, m % 2
                    dve.wait_ge(s_hi, b * 16 + 8 * p + m + 1)
                    tok = slice(g * 512, g * 512 + 512)
                    nc.vector.scalar_tensor_tensor(out=parts[:, 2 * k + 1, tok], in0=ps[:, m % 4, :],
                                                   scalar=b_qk[:, k, p:p + 1], in1=parts[:, 2 * k, tok],
                                                   op0=ALU.add, op1=ALU.subtract).then_inc(s_lo, 1)

            def clip0(b, c, n):
                h, g = n // NG, n % NG
                unit = b * (NC * UNITS0) + c * UNITS0 + n
                dve.wait_ge(s_s0, unit + 1)
                dve.wait_ge(s_e0, unit + 1)
                nc.vector.scalar_tensor_tensor(out=clipped_s[:, n % 2, :, :],
                                               in0=ps[:, 2 * (n % 2):2 * (n % 2) + 2, :], scalar=-CLIP,
                                               in1=clip_hi[:, bass.ds(2 * c, 2), g * 512:g * 512 + 512],
                                               op0=ALU.max, op1=ALU.min).then_inc(s_cl, 1)

            def scale0(b, c, n):
                unit = b * (NC * UNITS0) + c * UNITS0 + n
                o = ps[:, 4 + n % 4, 0:4 * DV].rearrange("p (t d) -> p t d", d=DV)
                dve.wait_ge(s_o0, unit + 3)
                nc.vector.reciprocal(rden[:, n % 4, :], o[:, :, D]).then_inc(s_rd, 1)
                dve.wait_ge(s_rd, unit + 1)
                dve.wait_ge(s_add, unit + 1)
                nc.vector.tensor_tensor(scaled[:, n % 4, :, :], o[:, :, 0:D],
                                        rden[:, n % 4, :].unsqueeze(2).to_broadcast([P, 4, D]),
                                        ALU.mult).then_inc(s_sc, 1)

            def chunk0(b, c, first):
                for n in range(UNITS0):
                    clip0(b, c, n)
                    if n >= 3:
                        scale0(b, c, n - 3)
                    elif not first:
                        scale0(b, c - 1, n - 3 + UNITS0)

            def norm_stats(b, r, src, ready):
                for t in range(NT):
                    ready(t)
                    nc.vector.bn_stats(stats[:, t, :], src[:, t, :]).then_inc(s_st, 1)
                dve.wait_ge(s_st, b * 3 * NT + (r + 1) * NT)
                dve.sem_inc(s_gate_v, 1)
                for t in range(NT):
                    last = nc.vector.bn_aggr(mv[:, t, :], stats[:, t, :])
                last.then_inc(s_ag, 1)
                dve.wait_ge(s_sq, b * 3 + r + 1)
                nc.vector.reciprocal(rstd[:, :], std[:, :]).then_inc(s_rs, 1)
                dve.wait_ge(s_rs, b * 3 + r + 1)

            def normalise(t, dst, src):
                return nc.vector.tensor_scalar(dst[:, t, :], src[:, t, :], mv[:, t, 0:1], rstd[:, t:t + 1],
                                               ALU.subtract, ALU.mult)

            def mask1(b, h, jj, k):
                unit = b * UNITS1 + h * NT + 2 * jj + k
                dve.wait_ge(s_re, unit + 3)
                dve.wait_ge(s_o1, unit + 1)
                nc.vector.scalar_tensor_tensor(out=probs1[:, k, :], in0=relu1[:, k, :],
                                               scalar=gat_x[:, h, bass.ds(2 * jj + k, 1)],
                                               in1=edge[:, bass.ds((2 * jj + k) * N, N)],
                                               op0=ALU.add, op1=ALU.mult).then_inc(s_m1, 1)

            def scale1(b, h):
                first = 4 * (h % 2)
                o = ps[:, first:first + 3, 0:SLOTS * DV].rearrange("p k (s d) -> p k s d", d=DV)
                dve.wait_ge(s_o1, b * UNITS1 + (h + 1) * NT + 2)
                den = gat_den[:, :].rearrange("p (k s) -> p k s", k=3)
                rd = gat_rden[:, :].rearrange("p (k s) -> p k s", k=3)
                pieces = ((0, 2, SLOTS), (2, 3, NT - 2 * SLOTS))
                for k0, k1, ns in pieces:
                    last = nc.vector.tensor_scalar(den[:, k0:k1, 0:ns], o[:, k0:k1, 0:ns, D], 1e-37, None, ALU.max)
                    last.then_inc(s_d1, 1)
                dve.wait_ge(s_d1, b * 3 * H + 3 * h + 2)
                nc.vector.reciprocal(gat_rden[:, 0:NT], gat_den[:, 0:NT]).then_inc(s_d1, 1)
                dve.wait_ge(s_d1, b * 3 * H + 3 * h + 3)
                for k0, k1, ns in pieces:
                    dst = ctxs[:, k0 * SLOTS:k0 * SLOTS + (k1 - k0) * ns, h * D:h * D + D].rearrange(
                        "p (k s) d -> p k s d", s=ns)
                    last = nc.vector.tensor_tensor(dst, o[:, k0:k1, 0:ns, 0:D],
                                                   rd[:, k0:k1, 0:ns].unsqueeze(3).to_broadcast([P, k1 - k0, ns, D]),
                                                   ALU.mult)
                last.then_inc(s_c1, 1)

            with dve.Fori(0, B) as b:
                turn(b, 0)
                low_parts(b, 0)
                for m in range(NC):
                    dve.wait_ge(s_v, b * NC + m + 1)
                    nc.vector.tensor_tensor(
                        v1_v[:, m, :, :, 0:D], ps[:, m % 4, :].rearrange("p (t h d) -> p h t d", t=2, h=H),
                        bv_all[:, :].rearrange("p (h d) -> p h d", h=H).unsqueeze(2).to_broadcast([P, H, 2, D]),
                        ALU.add).then_inc(s_vc, 1)
                low_parts(b, 1)
                chunk0(b, 0, True)
                with dve.Fori(1, NC) as c:
                    chunk0(b, c, False)
                for n in range(UNITS0 - 3, UNITS0):
                    scale0(b, NC - 1, n)
                turn(b, 1)
                dve.wait_ge(s_beta, b + 1)
                for m in range(NC):
                    dve.wait_ge(s_wo, b * NC + m + 1)
                    nc.vector.tensor_tensor(ctxs[:, 2 * m:2 * m + 2, :],
                                            ps[:, m % 4, :].rearrange("p (t f) -> p t f", t=2),
                                            x_keep[:, 2 * m:2 * m + 2, :], ALU.add).then_inc(s_r, 1)
                norm_stats(b, 0, ctxs, lambda t: dve.wait_ge(s_r, b * NC + t // 2 + 1))
                for t in range(NT):
                    nc.vector.scalar_tensor_tensor(out=ctxs[:, t, :], in0=ctxs[:, t, :], scalar=mv[:, t, 0:1],
                                                   in1=gamma_all[:, :], op0=ALU.subtract,
                                                   op1=ALU.mult).then_inc(s_z, 1)
                for t in range(NT):
                    dve.wait_ge(s_z, b * 2 * NT + t + 1)
                    nc.vector.scalar_tensor_tensor(out=ctxs[:, t, :], in0=ctxs[:, t, :], scalar=rstd[:, t:t + 1],
                                                   in1=x_keep[:, t, :], op0=ALU.mult, op1=ALU.add).then_inc(s_z, 1)
                norm_stats(b, 1, ctxs, lambda t: dve.wait_ge(s_z, b * 2 * NT + NT + t + 1))
                for t in range(NT):
                    last = normalise(t, x_keep, ctxs)
                    if t % 4 == 3:
                        last.then_inc(s_x1, 1)
                turn(b, 2)
                dve.wait_ge(s_sd, b * 4 + 1)
                bj = ps[:, 7, 0:NT * H].rearrange("p (t h) -> p h t", h=H)
                nc.vector.tensor_reduce(gat_max[:, :], bj, AX.X, ALU.max).then_inc(s_gv, 1)
                dve.wait_ge(s_sd, b * 4 + 2)
                nc.vector.tensor_reduce(gat_max4[:, :], ps[0:H, 6, 0:P], AX.X, ALU.max).then_inc(s_gv, 1)
                dve.wait_ge(s_gv, b * 8 + 2)
                nc.vector.tensor_scalar(gat_rbias[:, :], gat_max4[:, :], -0.8, SHIFT, ALU.mult,
                                        ALU.add).then_inc(s_gv, 1)
                nc.vector.tensor_scalar(gat_diag[:, :], ident[0:H, 0:H], gat_max4[:, 0:1], None,
                                        ALU.mult).then_inc(s_gv, 1)
                dve.wait_ge(s_sd, b * 4 + 3)
                nc.vector.tensor_copy(gat_b[:, :], ps[:, 5, 0:H]).then_inc(s_gv, 1)
                dve.wait_ge(s_gv, b * 8 + 5)
                nc.vector.tensor_tensor(gat_d[:, :, :], bj, gat_b[:, :].unsqueeze(2).to_broadcast([P, H, NT]),
                                        ALU.subtract).then_inc(s_gv, 1)
                dve.wait_ge(s_xy, b * 3 + 1)
                nc.vector.tensor_scalar(r_row, r_row, R_MAX, None, ALU.min).then_inc(s_rr, 1)
                dve.wait_ge(s_xy, b * 3 + 2)
                dve.wait_ge(s_edge, NT)
                nc.vector.tensor_scalar(gat_nx[:, :, :], gat_x[:, :, :], -1.0, None, ALU.mult).then_inc(s_gv, 2)
                for h in range(H):
                    mask1(b, h, 0, 0)
                    mask1(b, h, 0, 1)
                    if h >= 1:
                        scale1(b, h - 1)
                    with dve.Fori(1, NT // 2) as jj:
                        mask1(b, h, jj, 0)
                        mask1(b, h, jj, 1)
                scale1(b, H - 1)
                dve.wait_ge(s_x1m, b + 1)
                for g in range(NG):
                    s4 = slice(4 * g, 4 * g + 4)
                    dve.wait_ge(s_ee, b * NG + g + 1)
                    nc.vector.scalar_tensor_tensor(out=elu_e[:, s4, :], in0=elu_e[:, s4, :], scalar=1.0,
                                                   in1=x_keep[:, s4, :], op0=ALU.min, op1=ALU.add).then_inc(s_y, 1)
                    dve.wait_ge(s_y, b * 2 * NG + 2 * g + 1)
                    nc.vector.scalar_tensor_tensor(out=ctxs[:, s4, :], in0=ctxs[:, s4, :], scalar=0.0,
                                                   in1=elu_e[:, s4, :], op0=ALU.max, op1=ALU.add).then_inc(s_y, 1)
                norm_stats(b, 2, ctxs, lambda t: dve.wait_ge(s_y, b * 2 * NG + 2 * (t // 4) + 2))
                for t in range(NT):
                    last = normalise(t, ctxs, ctxs)
                    if t % 4 == 3:
                        last.then_inc(s_res, 1)


_INS = ['x', 'adj', 'L0_gnn_Wq', 'L0_gnn_bq', 'L0_gnn_Wk', 'L0_gnn_bk', 'L0_gnn_Wv', 'L0_gnn_bv', 'L0_gnn_Wo',
        'L0_gnn_bo', 'L0_gnn_gamma', 'L0_gnn_beta', 'L1_gnn_W', 'L1_gnn_a']


def kernel(**inputs):
    import numpy as _np
    import concourse.bacc as _bacc
    from concourse import mybir as _mybir
    from concourse.bass_utils import run_bass_kernel_spmd as _run

    nc = _bacc.Bacc("TRN2", target_bir_lowering=False, num_devices=1)
    arrays, args = {}, []
    for name in _INS:
        a = _np.ascontiguousarray(inputs[name])
        arrays[f"in_{name}_dram"] = a
        args.append(nc.dram_tensor(f"in_{name}_dram", a.shape, _mybir.dt.from_np(a.dtype), kind="ExternalInput").ap())
    args.append(nc.dram_tensor("out_0_dram", (B, N, F), F32, kind="ExternalOutput").ap())
    build(nc, *args)
    r = _run(nc, [arrays], core_ids=[0])
    return r.results[0]["out_0_dram"]
```

```python
from contextlib import ExitStack

import concourse.bass as bass
from concourse import mybir

ALU = mybir.AluOpType
ACT = mybir.ActivationFunctionType
AX = mybir.AxisListType
F32 = mybir.dt.float32
F16 = mybir.dt.float16
BF16 = mybir.dt.bfloat16
I32 = mybir.dt.int32
I8 = mybir.dt.int8

P = 128
B, N, F = 8, 2048, 256
H, D = 4, 64
CHUNK = 256
NC = N // CHUNK
NT = N // P
NG = N // 512
FT = F // P
DV = D + 1
CLIP = 80.0
EPS = 1e-5
SHIFT = 8.3177661667
DX = 2 * DV
HALF = N // 2
UNITS0 = H * NG
UNITS1 = 2 * H * NT
SLOTS = 3
GROUPS1 = 2 * H


def build(nc, x, adj, Wq, bq, Wk, bk, Wv, bv, Wo, bo, gamma, beta, W1, a1, out):
    with ExitStack() as ctx:
        def sb(name, shape, dt):
            return ctx.enter_context(nc.sbuf_tensor(name, shape, dt))

        def sem(name):
            return ctx.enter_context(nc.semaphore(name))

        clip_hi = sb("clip_hi", [P, NT, N], I8)
        edge = sb("edge", [P, NT * N], I8)
        x_keep = sb("x_keep", [P, NT, F], F32)
        reg_t = sb("reg_t", [P, 4096], F32)
        reg_c = sb("reg_c", [P, 4096], F32)
        reg_q = sb("reg_q", [P, NC * H * 2 * DX], F32)
        reg_k = sb("reg_k", [P, 4096], F32)
        v1 = sb("v1", [P, NC * H * 2 * DV], F32)
        w_t = sb("w_t", [P, 4, FT, F], F32)
        w1 = sb("w1", [P, FT, F], F32)
        wa = sb("wa", [P, FT, 2, H], F32)
        nz = sb("nz", [P, 2, N], BF16)
        b_qk = sb("b_qk", [P, 2, FT], F32)
        bv_all = sb("bv_all", [P, F], F32)
        gamma_all = sb("gamma_all", [P, F], F32)
        beta_all = sb("beta_all", [P, F], F32)
        bo_less_beta = sb("bo_less_beta", [1, F], F32)
        ident = sb("ident", [P, P], F32)
        ident_b = sb("ident_b", [P, P], BF16)
        ones = sb("ones", [4, P], F32)
        consts = sb("consts", [P, 2], F32)
        scaled = sb("scaled", [P, 4, 4, D], F32)
        rden = sb("rden", [P, 4, 4], F32)
        stats = sb("stats", [P, NT, 6], F32)
        mv = sb("mv", [P, NT, 2], F32)
        std = sb("std", [P, NT], F32)
        rstd = sb("rstd", [P, NT], F32)
        gat_max = sb("gat_max", [P, H], F32)
        gat_max4 = sb("gat_max4", [H, 1], F32)
        gat_diag = sb("gat_diag", [H, H], F32)
        gat_b = sb("gat_b", [P, H], F32)
        gat_nd = sb("gat_nd", [P, NC, H, 2], F32)
        gat_x = sb("gat_x", [P, NC, H, 2], F32)
        gat_y = sb("gat_y", [P, NC, H, 2], F32)
        gat_c = sb("gat_c", [P, NT, H], F32)
        gat_den = sb("gat_den", [P, NT // 2], F32)
        gat_rden = sb("gat_rden", [P, NT // 2], F32)

        x_t = reg_t[:, :].rearrange("p (f n) -> p f n", f=FT)
        clipped_s = reg_t[:, 0:2048].rearrange("p (u j n) -> p u j n", u=2, j=2)
        probs0 = reg_t[:, 2048:4096].rearrange("p (u j n) -> p u j n", u=2, j=2)
        edge_b = nz[:, :, :].rearrange("p u (j n) -> p u j n", j=NT)
        c_row = reg_k[0:H, 2048:4096]
        g_bufs = reg_t[:, 2048:4096].bitcast(BF16).rearrange("p (u n) -> p u n", u=4)
        ctxs = reg_c[:, :].rearrange("p (t f) -> p t f", f=F)
        parts = reg_c[:, :].bitcast(F16).rearrange("p (k n) -> p k n", k=4)
        w_nat = reg_c[:, 0:4 * FT * F].rearrange("p (w t f) -> p w t f", w=4, t=FT)
        a_all = reg_c[:, 2048:2048 + 2 * H * D].rearrange("p (h s d) -> p h s d", h=H, s=2)
        bo_row = reg_c[0:1, 3584:4096].rearrange("p (k f) -> p k f", k=2)
        gat_s = scaled[:, :, :, :].rearrange("p u t d -> p (u t d)")[:, 0:NT // 2 * DV].rearrange(
            "p (t d) -> p t d", d=DV)
        prods = reg_c[:, 0:3 * 2 * H * DX].rearrange("p (u g d) -> p u g d", u=3, d=DX)
        wa_prod = reg_c[:, 2560:2560 + FT * 2 * H * D].rearrange("p (t s h d) -> p t s h d", t=FT, s=2, h=H)
        q16 = reg_q[:, 0:8192].bitcast(F16).rearrange("p (k h n) -> p k h n", k=2, h=H)
        w_hi = reg_q[:, 0:NC * H * DX].bitcast(BF16)
        w_lo = reg_q[:, NC * H * DX:2 * NC * H * DX].bitcast(F16)
        elu_e = reg_q[:, 0:4096].rearrange("p (t f) -> p t f", f=F)
        k16 = reg_k[:, :].bitcast(F16)
        k16_v = k16.rearrange("p (c h n) -> p c h n", c=NC, h=H)
        c_all = reg_k[:, :].rearrange("p (u n) -> p u n", u=2)
        adj_rows = reg_k[:, :].bitcast(I32).rearrange("p (u n) -> p u n", u=2)
        v1_v = v1[:, :].rearrange("p (c h t d) -> p c h t d", c=NC, h=H, t=2)
        m_sum = v1[:, :].rearrange("p (t h d) -> p t h d", t=NT, h=H)

        ps = ctx.enter_context(nc.psum_tensor("ps", [P, 8, 512], F32))

        c_dram = nc.dram_tensor("c_scratch", (B, H, N), F32, kind="Internal").ap()

        s_w = sem("weights_loaded")
        s_adj = [sem(f"adj_loaded{i}") for i in range(2)]
        s_const = sem("consts_set")
        s_ones = sem("ones_set")
        s_setup = sem("setup_small")
        s_nz = sem("nz_made")
        s_adj_t = sem("adj_turned")
        s_clipm = sem("clip_hi_made")
        s_edge = sem("edge_made")
        s_wturn = sem("weights_turned")
        s_wcopy = sem("weights_copied")
        s_x = [sem(f"x_loaded{g}") for g in range(NG)]
        s_turn = sem("turn_filled")
        s_turn_a = sem("turn_copied_scalar")
        s_turn_v = sem("turn_copied_vector")
        s_qk = sem("qk_filled")
        s_hi = sem("hi_made")
        s_lo = sem("lo_made")
        s_v = sem("v_filled")
        s_vc = sem("v_copied")
        s_beta = sem("beta_added")
        s_stack = [sem(f"heads_stacked{i}") for i in range(FT)]
        s_s0 = sem("scores0_filled")
        s_cl = sem("scores0_clipped")
        s_e0 = sem("probs0_made")
        s_o0 = sem("ctx0_filled")
        s_rd = sem("rden_made")
        s_sc = sem("ctx0_scaled")
        s_add = sem("ctx0_added")
        s_zero = sem("ctx0_zeroed")
        s_wo = sem("wo_filled")
        s_r = sem("resid_made")
        s_st = sem("ln_stats")
        s_ag = sem("ln_aggregated")
        s_sq = sem("ln_std")
        s_rs = sem("ln_rstd")
        s_z = sem("ln_steps")
        s_x1 = sem("x1_made")
        s_wh = sem("wh_filled")
        s_whc = sem("wh_copied")
        s_ab = sem("gat_filled")
        s_gv = sem("gat_vector")
        s_xy = sem("gat_scalar")
        s_cr = sem("c_row_made")
        s_cs = sem("c_row_stored")
        s_cb = [sem(f"c_loaded{i}") for i in range(2)]
        s_pr = sem("products_made")
        s_wh_hi = sem("w_hi_made")
        s_wl = sem("w_lo_made")
        s_vones = sem("v_ones_set")
        s_eb = sem("edge_b_made")
        s_mf = sem("m_filled")
        s_ms = sem("m_sum_made")
        s_m1 = sem("g_made")
        s_o1 = sem("ctx1_filled")
        s_d1 = sem("den1_steps")
        s_c1 = sem("ctx1_scaled")
        s_x1m = sem("x1_less_one")
        s_ee = sem("elu_exp_made")
        s_y = sem("elu_steps")
        s_res = sem("result_made")
        s_out = sem("out_stored")

        s_gate_p = sem("pool_went_on")
        s_gate_v = sem("vector_went_on")

        block = ctx.enter_context(nc.Block())

        @block.sync
        def _(sp):
            for s, n in ((s_cl, 2), (s_e0, 2), (s_o0, 2), (s_sc, 4), (s_add, 4), (s_m1, 4), (s_o1, 4),
                         (s_c1, 2), (s_mf, 2), (s_ms, 2), (s_res, 1), (s_out, 16)):
                sp.sem_inc(s, n)
            for k, w in enumerate((Wq, Wk, Wv, Wo)):
                sp.dma_start(w_nat[:, k, :, :], w.rearrange("(t p) f -> p t f", p=P)).then_inc(s_w, 16)
            sp.dma_start(w1[:, :, :], W1.rearrange("(t p) f -> p t f", p=P)).then_inc(s_w, 16)
            sp.dma_start(a_all, a1.rearrange("h (s d) -> h s d", s=2).partition_broadcast(P)).then_inc(s_w, 16)
            for k, v in enumerate((bq, bk)):
                sp.dma_start(b_qk[:, k, :], v.rearrange("(t p) -> p t", p=P),
                             allow_slow_non_contiguous=True).then_inc(s_w, 16)
            for t, v in ((bv_all, bv), (gamma_all, gamma), (beta_all, beta)):
                sp.dma_start(t[:, :], v.partition_broadcast(P)).then_inc(s_w, 16)
            for k, v in enumerate((bo, beta)):
                sp.dma_start(bo_row[0:1, k, :], v.partition_broadcast(1)).then_inc(s_w, 16)
            for t in range(NT):
                if t >= 2:
                    sp.wait_ge(s_nz, t - 1)
                sp.dma_start(adj_rows[:, t % 2, :], adj[t * P:(t + 1) * P, :]).then_inc(s_adj[t % 2], 16)
            with sp.Fori(0, B) as b:
                sp.wait_ge(s_res, b * NG + 1)
                xb = x[bass.ds(b, 1), :, :].rearrange("o (t p) f -> p (o t) f", p=P)
                for g in range(NG):
                    sp.dma_start(x_keep[:, 4 * g:4 * g + 4, :], xb[:, 4 * g:4 * g + 4, :]).then_inc(s_x[g], 16)
                for p in range(FT):
                    sp.wait_ge(s_hi, b * 16 + 8 * (p + 1))
                    sp.wait_ge(s_lo, b * 16 + 8 * (p + 1))
                    for e in range(2):
                        h, rows = 2 * p + e, slice(D * e, D * e + D)
                        for k in range(2):
                            for half in (slice(0, D), slice(D, P)):
                                sp.dma_start(q16[half, k, h, :], parts[rows, k, :]).then_inc(s_stack[p], 16)
                            half = slice(D * k, D * k + D)
                            sp.dma_start(k16_v[half, :, h, :], parts[rows, 2 + k, :].rearrange(
                                "p (c n) -> p c n", c=NC)).then_inc(s_stack[p], 16)
                sp.wait_ge(s_cr, b + 1)
                cb = c_dram[bass.ds(b, 1), :, :]
                sp.dma_start(cb.rearrange("o h n -> (o h) n"), c_row).then_inc(s_cs, 16)
                sp.wait_ge(s_cs, 16 * b + 16)
                for h in range(H):
                    if h >= 2:
                        sp.wait_ge(s_m1, b * UNITS1 + (h - 1) * 2 * NT + 4)
                    row = cb[:, h, :].rearrange("o n -> (o n)").partition_broadcast(P)
                    sp.dma_start(c_all[:, h % 2, :], row).then_inc(s_cb[h % 2], 16)
                ob = out[bass.ds(b, 1), :, :].rearrange("o (t p) f -> p (o t) f", p=P)
                for g in range(NG):
                    sp.wait_ge(s_res, b * NG + g + 2)
                    sp.dma_start(ob[:, 4 * g:4 * g + 4, :], ctxs[:, 4 * g:4 * g + 4, :]).then_inc(s_out, 16)
            sp.wait_ge(s_out, 16 * NG * B + 16)

        @block.gpsimd
        def _(pool):
            nc.gpsimd.memset(ident[:, :], 0.0).then_inc(s_ones, 1)
            nc.gpsimd.memset(ones[:, :], 1.0).then_inc(s_ones, 1)
            nc.gpsimd.memset(consts[:, 0:1], EPS).then_inc(s_ones, 1)
            nc.gpsimd.memset(consts[:, 1:2], SHIFT).then_inc(s_ones, 1)
            pool.wait_ge(s_ones, 4)
            nc.gpsimd.affine_select(out=ident[:, :], in_=ident[:, :], compare_op=ALU.not_equal, fill=1.0,
                                    base=0, pattern=[[-1, P]], channel_multiplier=1).then_inc(s_ones, 1)
            pool.wait_ge(s_ones, 5)
            nc.gpsimd.tensor_copy(ident_b[:, :], ident[:, :]).then_inc(s_const, 1)
            pool.wait_ge(s_clipm, 2 * NT)
            for j in range(NT):
                nc.gpsimd.tensor_scalar(edge[:, j * N:j * N + N], clip_hi[:, j, :], 0.5 / CLIP, 0.5,
                                        ALU.mult, ALU.add).then_inc(s_edge, 1)
            with pool.Fori(0, B) as b:
                pool.wait_ge(s_c1, b * GROUPS1 + 2)
                pool.sem_inc(s_gate_p, 1)
                nc.gpsimd.memset(v1_v[:, :, :, :, D:DV].rearrange("p c h t d -> p (c h t) d"),
                                 1.0).then_inc(s_vones, 1)
                pool.wait_ge(s_turn, b * 24 + 8)
                pool.wait_ge(s_w, 16 * 13)
                nc.gpsimd.tensor_tensor(x_keep[:, :, :], x_keep[:, :, :],
                                        beta_all[:, :].unsqueeze(1).to_broadcast([P, NT, F]),
                                        ALU.add).then_inc(s_beta, 1)
                for p in range(FT):
                    pool.wait_ge(s_stack[p], (b + 1) * 192)
                pool.sem_inc(s_gate_p, 1)
                nc.gpsimd.memset(reg_c[:, :], 0.0).then_inc(s_zero, 1)
                pool.wait_ge(s_zero, b + 1)
                pool.sem_inc(s_gate_p, 1)
                with pool.Fori(0, NC) as c:
                    for n in range(UNITS0):
                        h, g = n // NG, n % NG
                        pool.wait_ge(s_sc, b * (NC * UNITS0) + c * UNITS0 + n + 5)
                        acc = ctxs[:, 4 * g:4 * g + 4, h * D:h * D + D]
                        nc.gpsimd.tensor_tensor(acc, acc, scaled[:, n % 4, :, :], ALU.add).then_inc(s_add, 1)
                pool.wait_ge(s_turn, b * 24 + 24)
                pool.sem_inc(s_gate_p, 1)
                nc.gpsimd.tensor_scalar(x_keep[:, :, :], x_keep[:, :, :], 1.0, -1.0,
                                        ALU.mult, ALU.add).then_inc(s_x1m, 1)

        @block.tensor
        def _(pe):
            pe.wait_ge(s_const, 1)
            pe.wait_ge(s_w, 16 * 13)
            for k in range(4):
                for f in range(FT):
                    m = k * FT + f
                    if m >= 4:
                        pe.wait_ge(s_wcopy, m - 3)
                    for t in range(FT):
                        last = nc.tensor.transpose(ps[:, m % 4, t * P:t * P + P],
                                                   w_nat[:, k, t, f * P:f * P + P], ident[:, :])
                    last.then_inc(s_wturn, 1)
            pe.wait_ge(s_wcopy, 4 * FT)
            for t in range(NT):
                pe.wait_ge(s_nz, t + 1)
                for half in range(2):
                    m = 2 * t + half
                    if m >= 4:
                        pe.wait_ge(s_clipm, m - 3)
                    bank = ps[:, m % 4, :].bitcast(BF16)
                    for j in range(8):
                        jt = 8 * half + j
                        last = nc.tensor.transpose(bank[:, j * P:j * P + P],
                                                   nz[:, t % 2, jt * P:jt * P + P], ident_b[:, :])
                    last.then_inc(s_adj_t, 1)
            pe.wait_ge(s_clipm, 2 * NT)

            def turn(b, r, src, ready):
                for m in range(2 * NG):
                    g, f = m // 2, m % 2
                    if f == 0:
                        ready(g)
                    if m >= 4:
                        pe.wait_ge(s_turn_v if f else s_turn_a, b * 12 + 4 * r + (m - 4) // 2 + 1)
                    for t in range(4):
                        last = nc.tensor.transpose(ps[:, m % 4, t * P:t * P + P],
                                                   src[:, 4 * g + t, f * P:f * P + P], ident[:, :])
                    last.then_inc(s_turn, 1)

            def turned(b, r):
                pe.wait_ge(s_turn_a, b * 12 + 4 * r + 4)
                pe.wait_ge(s_turn_v, b * 12 + 4 * r + 4)

            def tokens_by_features(m, bank, w, row=None):
                for t in range(2):
                    o = ps[:, bank, t * F:t * F + F]
                    tok = slice((2 * m + t) * P, (2 * m + t + 1) * P)
                    for f in range(FT):
                        last = nc.tensor.matmul(o, x_t[:, f, tok], w[:, f, :], start=(f == 0),
                                                stop=(f == FT - 1 and row is None))
                    if row is not None:
                        last = nc.tensor.matmul(o, ones[0:1, :], row, start=False, stop=True)
                return last

            def project_qk(b, p):
                for m in range(2 * NG):
                    g, k = m // 2, m % 2
                    if m >= 4:
                        pe.wait_ge(s_lo, b * 16 + 8 * p + m - 3)
                    for f in range(FT):
                        last = nc.tensor.matmul(ps[:, m % 4, :], w_t[:, k, f, p * P:p * P + P],
                                                x_t[:, f, g * 512:g * 512 + 512],
                                                start=(f == 0), stop=(f == FT - 1))
                    last.then_inc(s_qk, 1)

            def scores0(b, c, n):
                h, g = n // NG, n % NG
                pe.wait_ge(s_cl, b * (NC * UNITS0) + c * UNITS0 + n + 1)
                for j in range(2):
                    o = ps[:, 2 * (n % 2) + j, :]
                    keys = k16[:, bass.ds(c * (H * CHUNK) + h * CHUNK + j * P, P)]
                    for k in range(2):
                        last = nc.tensor.matmul(o, keys, q16[:, k, h, g * 512:g * 512 + 512],
                                                start=(k == 0), stop=(k == 1))
                last.then_inc(s_s0, 1)

            def context0(b, c, n):
                h = n // NG
                unit = b * (NC * UNITS0) + c * UNITS0 + n
                pe.wait_ge(s_e0, unit + 3)
                pe.wait_ge(s_sc, unit + 1)
                for j in range(2):
                    for t in range(4):
                        last = nc.tensor.matmul(
                            ps[:, 4 + n % 4, t * DV:t * DV + DV], probs0[:, n % 2, j, t * P:t * P + P],
                            v1[:, bass.ds(c * (2 * H * DV) + (2 * h + j) * DV, DV)],
                            start=(j == 0 and t == 0), stop=(j == 1), skip_group_check=True)
                last.then_inc(s_o0, 1)

            def chunk0(b, c, first):
                for n in range(UNITS0):
                    scores0(b, c, n)
                    if n >= 2:
                        context0(b, c, n - 2)
                    elif not first:
                        context0(b, c - 1, n - 2 + UNITS0)

            def sums1(b, g, q, k, first):
                h = g // 2
                pe.wait_ge(s_m1, b * UNITS1 + q * 4 + (g * NT + k + 5))
                cols = bass.ds(q * (4 * H * DX) + (k // 2 * 2 * H + 2 * h + k % 2) * DX, DX)
                for t in range(NT // 2):
                    o = ps[:, 3 * (g % 2) + t // SLOTS, t % SLOTS * DX:(t % SLOTS + 1) * DX]
                    for i, part in enumerate((w_hi, w_lo)):
                        last = nc.tensor.matmul(o, g_bufs[:, k, t * P:t * P + P], part[:, cols],
                                                start=(first and i == 0 and t % SLOTS == 0), stop=False,
                                                skip_group_check=True)
                last.then_inc(s_o1, 1)

            def m_step(b, u, q, g):
                step = b * NT + q * 2 + (8 * g + u)
                pe.wait_ge(s_eb, step + 1)
                pe.wait_ge(s_ms, step + 1)
                for j in range(NT):
                    for part in (w_hi, w_lo):
                        y = part.rearrange("p (c h t d) -> p c t h d", c=NC, h=H, t=2)[:, j // 2, j % 2, :, DV:DX]
                        last = nc.tensor.matmul(ps[:, 6 + u, 0:H * DV], edge_b[:, u, j, :], y,
                                                start=(j == 0 and part is w_hi), stop=(j == NT - 1 and part is w_lo))
                last.then_inc(s_mf, 1)

            def quad1(b, g, q, first):
                for k in range(4):
                    sums1(b, g, q, k, first and k == 0)
                    if g < 2 and k % 2 == 1:
                        m_step(b, k // 2, q, g)

            with pe.Fori(0, B) as b:
                pe.wait_ge(s_c1, b * GROUPS1 + 2)
                turn(b, 0, x_keep, lambda g: pe.wait_ge(s_x[g], 16 * b + 16))
                turned(b, 0)
                project_qk(b, 0)
                pe.wait_ge(s_lo, b * 16 + 8)
                for m in range(NC):
                    if m >= 4:
                        pe.wait_ge(s_vc, b * NC + m - 3)
                    tokens_by_features(m, m % 4, w_t[:, 2, :, :]).then_inc(s_v, 1)
                pe.wait_ge(s_vc, b * NC + NC)
                project_qk(b, 1)
                pe.wait_ge(s_lo, b * 16 + 16)
                pe.wait_ge(s_vones, b + 1)
                pe.wait_ge(s_stack[0], (b + 1) * 192)
                pe.wait_ge(s_stack[1], (b + 1) * 192)
                chunk0(b, 0, True)
                with pe.Fori(1, NC) as c:
                    chunk0(b, c, False)
                context0(b, NC - 1, UNITS0 - 2)
                context0(b, NC - 1, UNITS0 - 1)
                turn(b, 1, ctxs, lambda g: pe.wait_ge(s_add, (b + 1) * (NC * UNITS0) + 4) if g == 0 else None)
                turned(b, 1)
                for m in range(NC):
                    if m >= 4:
                        pe.wait_ge(s_r, b * NC + m - 3)
                    tokens_by_features(m, m % 4, w_t[:, 3, :, :], bo_less_beta[0:1, :]).then_inc(s_wo, 1)
                turn(b, 2, x_keep, lambda g: pe.wait_ge(s_x1, b * NG + g + 1))
                turned(b, 2)
                for t in range(NT):
                    for f in range(FT):
                        last = nc.tensor.matmul(ps[:, 7, t * 2 * H:(t + 1) * 2 * H], x_t[:, f, t * P:t * P + P],
                                                wa[:, f, :, :], start=(f == 0), stop=(f == FT - 1))
                last.then_inc(s_ab, 1)
                for g in range(NG):
                    for f in range(FT):
                        last = nc.tensor.matmul(ps[0:H, g, :], wa[:, f, 0, :], x_t[:, f, g * 512:g * 512 + 512],
                                                start=(f == 0), stop=(f == FT - 1))
                last.then_inc(s_ab, 1)
                for m in range(NC):
                    if m == 1:
                        pe.wait_ge(s_gv, b * 7 + 1)
                        nc.tensor.transpose(ps[0:H, 6, 0:P], gat_max[:, :], ident[:, :]).then_inc(s_ab, 1)
                    if m == 2:
                        pe.wait_ge(s_gv, b * 7 + 3)
                        nc.tensor.matmul(ps[:, 6, 256:256 + H], ones[0:H, :], gat_diag[:, :],
                                         start=True, stop=True).then_inc(s_ab, 1)
                    if m >= 2:
                        pe.wait_ge(s_whc, b * NC + m - 1)
                    tokens_by_features(m, 4 + m % 2, w1).then_inc(s_wh, 1)
                pe.wait_ge(s_wl, b * NC + NC)
                for g in range(GROUPS1):
                    pe.wait_ge(s_c1, b * GROUPS1 + g + 1)
                    quad1(b, g, 0, True)
                    with pe.Fori(1, NT // 4) as q:
                        quad1(b, g, q, False)

        @block.scalar
        def _(act):
            def turn(b, r):
                for g in range(NG):
                    act.wait_ge(s_turn, b * 24 + 8 * r + 2 * g + 1)
                    nc.scalar.activation(x_t[:, 0, g * 512:g * 512 + 512], ps[:, (2 * g) % 4, :],
                                         ACT.Copy).then_inc(s_turn_a, 1)

            def high_parts(b, p):
                for m in range(2 * NG):
                    g, k = m // 2, m % 2
                    act.wait_ge(s_qk, b * 16 + 8 * p + m + 1)
                    nc.scalar.activation(parts[:, 2 * k, g * 512:g * 512 + 512], ps[:, m % 4, :], ACT.Identity,
                                         bias=b_qk[:, k, p:p + 1]).then_inc(s_hi, 1)

            def exp0(b, c, n):
                unit = b * (NC * UNITS0) + c * UNITS0 + n
                act.wait_ge(s_cl, unit + 3)
                act.wait_ge(s_o0, unit + 1)
                nc.scalar.activation(probs0[:, n % 2, :, :], clipped_s[:, n % 2, :, :], ACT.Exp,
                                     scale=0.125).then_inc(s_e0, 1)

            def edges_b(b, t, u):
                act.wait_ge(s_mf, b * NT + t + 1)
                nc.scalar.activation(edge_b[:, u, :, :],
                                     edge[:, :].rearrange("p (j n) -> p j n", j=NT)[:, :, bass.ds(t * P, P)],
                                     ACT.Copy).then_inc(s_eb, 1)

            def m_copy(b, t, u):
                act.wait_ge(s_mf, b * NT + t + 3)
                nc.scalar.activation(v1[:, bass.ds(t * (H * DV), H * DV)], ps[:, 6 + u, 0:H * DV],
                                     ACT.Copy).then_inc(s_ms, 1)

            with act.Fori(0, B) as b:
                turn(b, 0)
                act.wait_ge(s_out, 16 * NG * b + 16)
                act.wait_ge(s_w, 16 * 13)
                high_parts(b, 0)
                act.wait_ge(s_stack[0], (b + 1) * 192)
                high_parts(b, 1)
                with act.Fori(0, NC) as c:
                    for n in range(UNITS0):
                        exp0(b, c, n)
                turn(b, 1)
                for r in range(2):
                    act.wait_ge(s_ag, b * 3 + r + 1)
                    nc.scalar.activation(std[:, :], mv[:, :, 1], ACT.Sqrt, bias=consts[:, 0:1]).then_inc(s_sq, 1)
                turn(b, 2)
                act.wait_ge(s_gv, b * 7 + 2)
                act.wait_ge(s_ab, b * 4 + 2)
                nc.scalar.activation(c_row.rearrange("h (g n) -> h g n", g=NG), ps[0:H, 0:NG, :], ACT.Identity,
                                     bias=gat_max4[:, :]).then_inc(s_cr, 1)

                def wh_copy(m):
                    act.wait_ge(s_wh, b * NC + m + 1)
                    nc.scalar.activation(v1_v[:, m, :, :, 0:D],
                                         ps[:, 4 + m % 2, :].rearrange("p (t h d) -> p h t d", t=2, h=H),
                                         ACT.Copy).then_inc(s_whc, 1)

                for m in range(3):
                    wh_copy(m)
                act.wait_ge(s_gv, b * 7 + 6)
                nc.scalar.activation(gat_x[:, :, :, :], gat_nd[:, :, :, :], ACT.Exp, scale=-1.0,
                                     bias=consts[:, 1:2]).then_inc(s_xy, 1)
                nc.scalar.activation(gat_y[:, :, :, :], gat_nd[:, :, :, :], ACT.Exp, scale=-0.2,
                                     bias=consts[:, 1:2]).then_inc(s_xy, 1)
                nc.scalar.activation(gat_c[:, :, :], gat_c[:, :, :], ACT.Exp, scale=-0.8).then_inc(s_xy, 1)
                for m in range(3, NC):
                    wh_copy(m)
                for c in range(NC):
                    act.wait_ge(s_pr, b * 2 * NC + 2 * c + 2)
                    nc.scalar.activation(w_hi[:, c * (2 * H * DX):(c + 1) * (2 * H * DX)],
                                         prods[:, c % 3, :, :].rearrange("p g d -> p (g d)"),
                                         ACT.Copy).then_inc(s_wh_hi, 1)
                act.wait_ge(s_edge, NT)
                edges_b(b, 0, 0)
                edges_b(b, 1, 1)
                with act.Fori(0, NT // 2 - 1) as p:
                    for u in range(2):
                        m_copy(b, 2 * p + u, u)
                        edges_b(b, 2 * p + u + 2, u)
                for u in range(2):
                    m_copy(b, NT - 2 + u, u)
                for g in range(NG):
                    act.wait_ge(s_c1, b * GROUPS1 + GROUPS1 + 2)
                    nc.scalar.activation(elu_e[:, 4 * g:4 * g + 4, :], ctxs[:, 4 * g:4 * g + 4, :],
                                         ACT.Exp).then_inc(s_ee, 1)
                act.wait_ge(s_ag, b * 3 + 3)
                nc.scalar.activation(std[:, :], mv[:, :, 1], ACT.Sqrt, bias=consts[:, 0:1]).then_inc(s_sq, 1)

        @block.vector
        def _(dve):
            dve.wait_ge(s_w, 16 * 13)
            for f in range(FT):
                for s in range(2):
                    nc.vector.tensor_tensor(wa_prod[:, f, s, :, :], w1[:, f, :].rearrange("p (h d) -> p h d", h=H),
                                            a_all[:, :, s, :], ALU.mult).then_inc(s_setup, 1)
            nc.vector.tensor_tensor(bo_less_beta[:, :], bo_row[:, 0, :], bo_row[:, 1, :],
                                    ALU.subtract).then_inc(s_setup, 1)
            dve.wait_ge(s_setup, 5)
            for f in range(FT):
                for s in range(2):
                    nc.vector.tensor_reduce(wa[:, f, s, :], wa_prod[:, f, s, :, :], AX.X, ALU.add).then_inc(s_setup, 1)
            for m in range(4 * FT):
                dve.wait_ge(s_wturn, m + 1)
                nc.vector.tensor_copy(w_t[:, m // FT, m % FT, :], ps[:, m % 4, 0:F]).then_inc(s_wcopy, 1)
            def marks(t):
                dve.wait_ge(s_adj[t % 2], 16 * (t // 2) + 16)
                if t >= 2:
                    dve.wait_ge(s_adj_t, 2 * (t - 1))
                nc.vector.tensor_scalar(nz[:, t % 2, :], adj_rows[:, t % 2, :], 0.0, None,
                                        ALU.not_equal).then_inc(s_nz, 1)

            marks(0)
            for t in range(NT):
                if t + 1 < NT:
                    marks(t + 1)
                for half in range(2):
                    m = 2 * t + half
                    dve.wait_ge(s_adj_t, m + 1)
                    nc.vector.tensor_scalar(clip_hi[:, 8 * half:8 * half + 8, t * P:t * P + P],
                                            ps[:, m % 4, :].bitcast(BF16).rearrange("p (j n) -> p j n", j=8),
                                            2 * CLIP, -CLIP, ALU.mult, ALU.add).then_inc(s_clipm, 1)
            dve.wait_ge(s_clipm, 2 * NT)
            dve.wait_ge(s_setup, 9)

            def turn(b, r):
                for g in range(NG):
                    dve.wait_ge(s_turn, b * 24 + 8 * r + 2 * g + 2)
                    nc.vector.tensor_copy(x_t[:, 1, g * 512:g * 512 + 512],
                                          ps[:, (2 * g + 1) % 4, :]).then_inc(s_turn_v, 1)

            def low_parts(b, p):
                for m in range(2 * NG):
                    g, k = m // 2, m % 2
                    dve.wait_ge(s_hi, b * 16 + 8 * p + m + 1)
                    tok = slice(g * 512, g * 512 + 512)
                    nc.vector.scalar_tensor_tensor(out=parts[:, 2 * k + 1, tok], in0=ps[:, m % 4, :],
                                                   scalar=b_qk[:, k, p:p + 1], in1=parts[:, 2 * k, tok],
                                                   op0=ALU.add, op1=ALU.subtract).then_inc(s_lo, 1)

            def clip0(b, c, n):
                h, g = n // NG, n % NG
                unit = b * (NC * UNITS0) + c * UNITS0 + n
                dve.wait_ge(s_s0, unit + 1)
                dve.wait_ge(s_e0, unit + 1)
                nc.vector.scalar_tensor_tensor(out=clipped_s[:, n % 2, :, :],
                                               in0=ps[:, 2 * (n % 2):2 * (n % 2) + 2, :], scalar=-CLIP,
                                               in1=clip_hi[:, bass.ds(2 * c, 2), g * 512:g * 512 + 512],
                                               op0=ALU.max, op1=ALU.min).then_inc(s_cl, 1)

            def scale0(b, c, n):
                unit = b * (NC * UNITS0) + c * UNITS0 + n
                o = ps[:, 4 + n % 4, 0:4 * DV].rearrange("p (t d) -> p t d", d=DV)
                dve.wait_ge(s_o0, unit + 3)
                nc.vector.reciprocal(rden[:, n % 4, :], o[:, :, D]).then_inc(s_rd, 1)
                dve.wait_ge(s_rd, unit + 1)
                dve.wait_ge(s_add, unit + 1)
                nc.vector.tensor_tensor(scaled[:, n % 4, :, :], o[:, :, 0:D],
                                        rden[:, n % 4, :].unsqueeze(2).to_broadcast([P, 4, D]),
                                        ALU.mult).then_inc(s_sc, 1)

            def chunk0(b, c, first):
                for n in range(UNITS0):
                    clip0(b, c, n)
                    if n >= 3:
                        scale0(b, c, n - 3)
                    elif not first:
                        scale0(b, c - 1, n - 3 + UNITS0)

            def norm_stats(b, r, src, ready):
                for t in range(NT):
                    ready(t)
                    nc.vector.bn_stats(stats[:, t, :], src[:, t, :]).then_inc(s_st, 1)
                dve.wait_ge(s_st, b * 3 * NT + (r + 1) * NT)
                dve.sem_inc(s_gate_v, 1)
                for t in range(NT):
                    last = nc.vector.bn_aggr(mv[:, t, :], stats[:, t, :])
                last.then_inc(s_ag, 1)
                dve.wait_ge(s_sq, b * 3 + r + 1)
                nc.vector.reciprocal(rstd[:, :], std[:, :]).then_inc(s_rs, 1)
                dve.wait_ge(s_rs, b * 3 + r + 1)

            def normalise(t, dst, src):
                return nc.vector.tensor_scalar(dst[:, t, :], src[:, t, :], mv[:, t, 0:1], rstd[:, t:t + 1],
                                               ALU.subtract, ALU.mult)

            def mask1(b, g, q, k):
                h, half = g // 2, g % 2
                dve.wait_ge(s_o1, b * UNITS1 + q * 4 + (g * NT + k + 1))
                nd = gat_nd[:, :, :, :].rearrange("p c h t -> p (c h t)")
                nc.vector.scalar_tensor_tensor(out=g_bufs[:, k, :],
                                               in0=c_all[:, h % 2, half * HALF:half * HALF + HALF],
                                               scalar=nd[:, bass.ds(q * (4 * H) + (k // 2 * 2 * H + 2 * h + k % 2), 1)],
                                               in1=edge[:, bass.ds(q * (4 * N) + (k * N + half * HALF), HALF)],
                                               op0=ALU.is_gt, op1=ALU.mult).then_inc(s_m1, 1)

            def scale1(b, g):
                h, half = g // 2, g % 2
                tiles = slice(half * NT // 2, (half + 1) * NT // 2)
                o = ps[:, 3 * half:3 * half + 3, 0:SLOTS * DX].rearrange("p k (s d) -> p k s d", d=DX)
                pieces = ((0, 2, SLOTS), (2, 3, NT // 2 - 2 * SLOTS))
                dve.wait_ge(s_o1, b * UNITS1 + (g + 1) * NT + 4)
                dve.wait_ge(s_ms, b * NT + (half + 1) * NT // 2 + 2)
                step = b * 7 * GROUPS1 + 7 * g
                for k0, k1, ns in pieces:
                    t0 = k0 * SLOTS
                    piece = slice(t0, t0 + (k1 - k0) * ns)
                    m = m_sum[:, half * NT // 2 + t0:half * NT // 2 + t0 + (k1 - k0) * ns, h, :]
                    nc.vector.tensor_tensor(gat_s[:, piece, :].rearrange("p (k s) d -> p k s d", s=ns),
                                            m.rearrange("p (k s) d -> p k s d", s=ns), o[:, k0:k1, 0:ns, DV:DX],
                                            ALU.subtract).then_inc(s_d1, 1)
                dve.wait_ge(s_d1, step + 2)
                nc.vector.tensor_tensor(gat_s[:, :, :], gat_s[:, :, :],
                                        gat_c[:, tiles, h].unsqueeze(2).to_broadcast([P, NT // 2, DV]),
                                        ALU.mult).then_inc(s_d1, 1)
                dve.wait_ge(s_d1, step + 3)
                for k0, k1, ns in pieces:
                    t0 = k0 * SLOTS
                    gs = gat_s[:, t0:t0 + (k1 - k0) * ns, :].rearrange("p (k s) d -> p k s d", s=ns)
                    nc.vector.tensor_tensor(gs, o[:, k0:k1, 0:ns, 0:DV], gs, ALU.add).then_inc(s_d1, 1)
                dve.wait_ge(s_d1, step + 5)
                nc.vector.tensor_scalar(gat_den[:, :], gat_s[:, :, D], 1e-37, None, ALU.max).then_inc(s_d1, 1)
                dve.wait_ge(s_d1, step + 6)
                nc.vector.reciprocal(gat_rden[:, :], gat_den[:, :]).then_inc(s_d1, 1)
                dve.wait_ge(s_d1, step + 7)
                nc.vector.tensor_tensor(ctxs[:, tiles, h * D:h * D + D], gat_s[:, :, 0:D],
                                        gat_rden[:, :].unsqueeze(2).to_broadcast([P, NT // 2, D]),
                                        ALU.mult).then_inc(s_c1, 1)

            with dve.Fori(0, B) as b:
                turn(b, 0)
                low_parts(b, 0)
                for m in range(NC):
                    dve.wait_ge(s_v, b * NC + m + 1)
                    nc.vector.tensor_tensor(
                        v1_v[:, m, :, :, 0:D], ps[:, m % 4, :].rearrange("p (t h d) -> p h t d", t=2, h=H),
                        bv_all[:, :].rearrange("p (h d) -> p h d", h=H).unsqueeze(2).to_broadcast([P, H, 2, D]),
                        ALU.add).then_inc(s_vc, 1)
                low_parts(b, 1)
                chunk0(b, 0, True)
                with dve.Fori(1, NC) as c:
                    chunk0(b, c, False)
                for n in range(UNITS0 - 3, UNITS0):
                    scale0(b, NC - 1, n)
                turn(b, 1)
                dve.wait_ge(s_beta, b + 1)
                for m in range(NC):
                    dve.wait_ge(s_wo, b * NC + m + 1)
                    nc.vector.tensor_tensor(ctxs[:, 2 * m:2 * m + 2, :],
                                            ps[:, m % 4, :].rearrange("p (t f) -> p t f", t=2),
                                            x_keep[:, 2 * m:2 * m + 2, :], ALU.add).then_inc(s_r, 1)
                norm_stats(b, 0, ctxs, lambda t: dve.wait_ge(s_r, b * NC + t // 2 + 1))
                for t in range(NT):
                    nc.vector.scalar_tensor_tensor(out=ctxs[:, t, :], in0=ctxs[:, t, :], scalar=mv[:, t, 0:1],
                                                   in1=gamma_all[:, :], op0=ALU.subtract,
                                                   op1=ALU.mult).then_inc(s_z, 1)
                for t in range(NT):
                    dve.wait_ge(s_z, b * 2 * NT + t + 1)
                    nc.vector.scalar_tensor_tensor(out=ctxs[:, t, :], in0=ctxs[:, t, :], scalar=rstd[:, t:t + 1],
                                                   in1=x_keep[:, t, :], op0=ALU.mult, op1=ALU.add).then_inc(s_z, 1)
                norm_stats(b, 1, ctxs, lambda t: dve.wait_ge(s_z, b * 2 * NT + NT + t + 1))
                for t in range(NT):
                    last = normalise(t, x_keep, ctxs)
                    if t % 4 == 3:
                        last.then_inc(s_x1, 1)
                turn(b, 2)
                dve.wait_ge(s_ab, b * 4 + 1)
                ab = ps[:, 7, 0:NT * 2 * H]
                nc.vector.tensor_reduce(gat_max[:, :], ab.rearrange("p (t s h) -> p s h t", s=2, h=H)[:, 1, :, :],
                                        AX.X, ALU.max).then_inc(s_gv, 1)
                dve.wait_ge(s_ab, b * 4 + 3)
                nc.vector.tensor_reduce(gat_max4[:, :], ps[0:H, 6, 0:P], AX.X, ALU.max).then_inc(s_gv, 1)
                dve.wait_ge(s_gv, b * 7 + 2)
                nc.vector.tensor_scalar(gat_diag[:, :], ident[0:H, 0:H], gat_max4[:, 0:1], None,
                                        ALU.mult).then_inc(s_gv, 1)
                dve.wait_ge(s_ab, b * 4 + 4)
                nc.vector.tensor_copy(gat_b[:, :], ps[:, 6, 256:256 + H]).then_inc(s_gv, 1)
                dve.wait_ge(s_gv, b * 7 + 4)
                b_cht = ab.rearrange("p (c t s h) -> p s c h t", c=NC, t=2, s=2)[:, 1, :, :, :]
                nc.vector.tensor_tensor(gat_nd[:, :, :, :],
                                        gat_b[:, :].unsqueeze(1).unsqueeze(3).to_broadcast([P, NC, H, 2]), b_cht,
                                        ALU.subtract).then_inc(s_gv, 1)
                nc.vector.tensor_tensor(gat_c[:, :, :], ab.rearrange("p (t s h) -> p s t h", s=2, h=H)[:, 0, :, :],
                                        gat_b[:, :].unsqueeze(1).to_broadcast([P, NT, H]), ALU.add).then_inc(s_gv, 1)
                dve.wait_ge(s_xy, b * 3 + 3)
                nc.vector.tensor_scalar(gat_c[:, :, :], gat_c[:, :, :], 1.0, None, ALU.min).then_inc(s_gv, 1)

                def products(c):
                    dve.wait_ge(s_whc, b * NC + c + 1)
                    if c >= 3:
                        dve.wait_ge(s_wl, b * NC + c - 2)
                    w = v1[:, :].rearrange("p (g d) -> p g d", d=DV)[:, 2 * H * c:2 * H * (c + 1), :]
                    for i, f in enumerate((gat_x, gat_y)):
                        nc.vector.tensor_tensor(prods[:, c % 3, :, i * DV:(i + 1) * DV], w,
                                                f[:, c, :, :].rearrange("p h t -> p (h t)").unsqueeze(2)
                                                .to_broadcast([P, 2 * H, DV]), ALU.mult).then_inc(s_pr, 1)

                def low_of_products(c):
                    dve.wait_ge(s_wh_hi, b * NC + c + 1)
                    cols = slice(c * (2 * H * DX), (c + 1) * (2 * H * DX))
                    nc.vector.tensor_tensor(w_lo[:, cols], prods[:, c % 3, :, :].rearrange("p g d -> p (g d)"),
                                            w_hi[:, cols], ALU.subtract).then_inc(s_wl, 1)

                for c in range(NC):
                    products(c)
                    if c >= 2:
                        low_of_products(c - 2)
                low_of_products(NC - 2)
                low_of_products(NC - 1)
                for g in range(GROUPS1):
                    if g % 2 == 0:
                        dve.wait_ge(s_cb[g // 2 % 2], 32 * b + 16 * (g // 4) + 16)
                    for k in range(4):
                        mask1(b, g, 0, k)
                    if g >= 1:
                        scale1(b, g - 1)
                    with dve.Fori(1, NT // 4) as q:
                        for k in range(4):
                            mask1(b, g, q, k)
                scale1(b, GROUPS1 - 1)
                dve.wait_ge(s_x1m, b + 1)
                for g in range(NG):
                    s4 = slice(4 * g, 4 * g + 4)
                    dve.wait_ge(s_ee, b * NG + g + 1)
                    nc.vector.scalar_tensor_tensor(out=elu_e[:, s4, :], in0=elu_e[:, s4, :], scalar=1.0,
                                                   in1=x_keep[:, s4, :], op0=ALU.min, op1=ALU.add).then_inc(s_y, 1)
                    dve.wait_ge(s_y, b * 2 * NG + 2 * g + 1)
                    nc.vector.scalar_tensor_tensor(out=ctxs[:, s4, :], in0=ctxs[:, s4, :], scalar=0.0,
                                                   in1=elu_e[:, s4, :], op0=ALU.max, op1=ALU.add).then_inc(s_y, 1)
                norm_stats(b, 2, ctxs, lambda t: dve.wait_ge(s_y, b * 2 * NG + 2 * (t // 4) + 2))
                for t in range(NT):
                    last = normalise(t, ctxs, ctxs)
                    if t % 4 == 3:
                        last.then_inc(s_res, 1)


_INS = ['x', 'adj', 'L0_gnn_Wq', 'L0_gnn_bq', 'L0_gnn_Wk', 'L0_gnn_bk', 'L0_gnn_Wv', 'L0_gnn_bv', 'L0_gnn_Wo',
        'L0_gnn_bo', 'L0_gnn_gamma', 'L0_gnn_beta', 'L1_gnn_W', 'L1_gnn_a']


def kernel(**inputs):
    import numpy as _np
    import concourse.bacc as _bacc
    from concourse import mybir as _mybir
    from concourse.bass_utils import run_bass_kernel_spmd as _run

    nc = _bacc.Bacc("TRN2", target_bir_lowering=False, num_devices=1)
    arrays, args = {}, []
    for name in _INS:
        a = _np.ascontiguousarray(inputs[name])
        arrays[f"in_{name}_dram"] = a
        args.append(nc.dram_tensor(f"in_{name}_dram", a.shape, _mybir.dt.from_np(a.dtype), kind="ExternalInput").ap())
    args.append(nc.dram_tensor("out_0_dram", (B, N, F), F32, kind="ExternalOutput").ap())
    build(nc, *args)
    r = _run(nc, [arrays], core_ids=[0])
    return r.results[0]["out_0_dram"]
```

```python
from contextlib import ExitStack

import concourse.bass as bass
from concourse import mybir

ALU = mybir.AluOpType
ACT = mybir.ActivationFunctionType
AX = mybir.AxisListType
F32 = mybir.dt.float32
F16 = mybir.dt.float16
BF16 = mybir.dt.bfloat16
I32 = mybir.dt.int32
I8 = mybir.dt.int8

P = 128
B, N, F = 8, 2048, 256
H, D = 4, 64
CHUNK = 256
NC = N // CHUNK
NT = N // P
NG = N // 512
FT = F // P
DV = D + 1
CLIP = 80.0
EPS = 1e-5
SHIFT0 = 5.84
SHIFT = 8.3177661667
DX = 2 * DV
HALF = N // 2
CTX_LAG, DEN_LAG, ADD_LAG = 3, 4, 5
UNITS0 = H * NG
UNITS1 = 2 * H * NT
TURNS = ((2, 3, 0, 1), (0, 1, 2, 3), (0, 1, 2, 3))
PREP_BANKS = (0, 1, 2, 6)
STACKED = 16 * 2 * 2 * 2
SLOTS = 3
GROUPS1 = 2 * H
M_STEPS = GROUPS1 * NT // 2


def build(nc, x, adj, Wq, bq, Wk, bk, Wv, bv, Wo, bo, gamma, beta, W1, a1, out):
    with ExitStack() as ctx:
        def sb(name, shape, dt):
            return ctx.enter_context(nc.sbuf_tensor(name, shape, dt))

        def sem(name):
            return ctx.enter_context(nc.semaphore(name))

        clip_hi = sb("clip_hi", [P, NT, N], I8)
        edge = sb("edge", [P, NT * N], I8)
        x_keep = sb("x_keep", [P, NT, F], F32)
        reg_t = sb("reg_t", [P, 4096], F32)
        reg_c = sb("reg_c", [P, 4096], F32)
        reg_q = sb("reg_q", [P, NC * H * 2 * DX], F32)
        reg_k = sb("reg_k", [P, 4096], F32)
        v1 = sb("v1", [P, NC * H * 2 * DV], F32)
        w_t = sb("w_t", [P, 4, FT, F], F32)
        w1 = sb("w1", [P, FT, F], F32)
        wa = sb("wa", [P, FT, 2, H], F32)
        nz = sb("nz", [P, 2, N], BF16)
        b_qk = sb("b_qk", [P, 3, FT], F32)
        gamma_all = sb("gamma_all", [P, F], F32)
        beta_all = sb("beta_all", [P, F], F32)
        bias_row = sb("bias_row", [1, F], F32)
        ident = sb("ident", [P, P], F32)
        ident_b = sb("ident_b", [P, P], BF16)
        ones = sb("ones", [4, P], F32)
        consts = sb("consts", [P, 4], F32)
        scaled = sb("scaled", [P, 4, 4, D], F32)
        rden = sb("rden", [P, 4, 4], F32)
        stats = sb("stats", [P, NT, 6], F32)
        mv = sb("mv", [P, NT, 2], F32)
        std = sb("std", [P, NT], F32)
        rstd = sb("rstd", [P, NT], F32)
        gat_max = sb("gat_max", [P, H], F32)
        gat_max4 = sb("gat_max4", [H, 1], F32)
        gat_diag = sb("gat_diag", [H, H], F32)
        gat_b = sb("gat_b", [P, H], F32)
        gat_nd = sb("gat_nd", [P, NC, H, 2], F32)
        gat_x = sb("gat_x", [P, NC, H, 2], F32)
        gat_y = sb("gat_y", [P, NC, H, 2], F32)
        gat_c = sb("gat_c", [P, H, NT], F32)
        gat_den = sb("gat_den", [P, NT // 2], F32)
        gat_rden = sb("gat_rden", [P, NT // 2], F32)

        x_t = reg_t[:, :].rearrange("p (g f n) -> p g f n", g=NG, f=FT)
        x_in = [r[:, i * 1024:(i + 1) * 1024].rearrange("p (t f) -> p t f", f=F)
                for r, i in ((reg_t, 0), (reg_t, 1), (reg_k, 2), (reg_k, 3))]
        probs0 = reg_t[:, :].rearrange("p (u j n) -> p u j n", u=4, j=2)
        probs0_hi = reg_t[:, :].bitcast(BF16).rearrange("p (u j n w) -> p u j n w", u=4, j=2, w=2)[:, :, :, :, 1]
        probs0_lo = nz[:, :, :].rearrange("p u n -> p (u n)").bitcast(F16).rearrange(
            "p (u j n) -> p u j n", u=4, j=2)
        edge_b = nz[:, :, :].rearrange("p u (j n) -> p u j n", j=NT)
        elu_e = nz[:, :, :].rearrange("p u n -> p (u n)").bitcast(F32).rearrange("p (u t f) -> p u t f", u=2, f=F)
        c_t = reg_k[0:H * NT, 2 * HALF:2 * HALF + P]
        g_bufs = reg_t[:, 2048:4096].bitcast(BF16).rearrange("p (u n) -> p u n", u=4)
        ctxs = reg_c[:, :].rearrange("p (t f) -> p t f", f=F)
        parts = reg_c[:, :].bitcast(F16).rearrange("p (k n) -> p k n", k=4)
        w_nat = reg_c[:, 0:4 * FT * F].rearrange("p (w t f) -> p w t f", w=4, t=FT)
        a_all = reg_c[:, 2048:2048 + 2 * H * D].rearrange("p (h s d) -> p h s d", h=H, s=2)
        bo_row = reg_c[0:1, 3584:4096].rearrange("p (k f) -> p k f", k=2)
        gat_s = scaled[:, :, :, :].rearrange("p u t d -> p (u t d)")[:, 0:NT // 2 * DV].rearrange(
            "p (t d) -> p t d", d=DV)
        prods = reg_c[:, 0:3 * 2 * H * DX].rearrange("p (u g d) -> p u g d", u=3, d=DX)
        wa_prod = reg_c[:, 2560:2560 + FT * 2 * H * D].rearrange("p (t s h d) -> p t s h d", t=FT, s=2, h=H)
        q16 = reg_q[:, 0:8192].bitcast(F16).rearrange("p (k h n) -> p k h n", k=2, h=H)
        w_hi = reg_q[:, 0:NC * H * DX].bitcast(BF16)
        w_lo = reg_q[:, NC * H * DX:2 * NC * H * DX].bitcast(F16)
        k16 = reg_k[:, :].bitcast(F16)
        k16_v = k16.rearrange("p (c h n) -> p c h n", c=NC, h=H)
        c_all = reg_k[:, 0:2 * HALF].rearrange("p (u n) -> p u n", u=2)
        adj_rows = reg_k[:, :].bitcast(I32).rearrange("p (u n) -> p u n", u=2)
        v_hi = v1[:, 0:NC * H * DV].bitcast(BF16)
        v_lo = v1[:, NC * H * DV:NC * H * DV + NC * H * D].bitcast(F16)
        v_hi_v = v_hi.rearrange("p (c h t d) -> p c h t d", c=NC, h=H, t=2)
        v_lo_v = v_lo.rearrange("p (c h t d) -> p c h t d", c=NC, h=H, t=2)
        v1_v = v1[:, :].rearrange("p (c h t d) -> p c h t d", c=NC, h=H, t=2)
        m_sum = v1[:, :].rearrange("p (t h d) -> p t h d", t=NT, h=H)

        ps = ctx.enter_context(nc.psum_tensor("ps", [P, 8, 512], F32))

        c_dram = nc.dram_tensor("c_scratch", (B, H, N), F32, kind="Internal").ap()

        s_w = sem("weights_loaded")
        s_adj = [sem(f"adj_loaded{i}") for i in range(2)]
        s_const = sem("consts_set")
        s_ones = sem("ones_set")
        s_setup = sem("setup_small")
        s_nz = sem("nz_made")
        s_adj_t = sem("adj_turned")
        s_clip_v = sem("clip_hi_made_by_vector")
        s_clip_s = sem("clip_hi_made_by_scalar")
        s_edge = sem("edge_made")
        s_wturn = sem("weights_turned")
        s_wcopy = sem("weights_copied")
        s_x = [sem(f"x_loaded{g}") for g in range(NG)]
        s_turn = sem("turn_filled")
        s_turn_c = sem("turn_copied")
        s_qk = sem("qk_filled")
        s_hi = sem("hi_made")
        s_lo = sem("lo_made")
        s_v = sem("v_filled")
        s_vh = sem("v_hi_made")
        s_vc = sem("v_lo_made")
        s_lo_v = sem("probs0_low_by_vector")
        s_lo_p = sem("probs0_low_by_pool")
        s_bias = sem("bias_filled")
        s_xk = sem("x_kept")
        s_beta = sem("beta_added")
        s_stack = [[sem(f"heads_stacked{i}_{t}") for t in range(2)] for i in range(FT)]
        s_s0 = sem("scores0_filled")
        s_cl = sem("scores0_clipped")
        s_e0 = sem("probs0_made")
        s_o0 = sem("ctx0_filled")
        s_rd = sem("rden_made")
        s_sc = sem("ctx0_scaled")
        s_add = sem("ctx0_added")
        s_wo = sem("wo_filled")
        s_r = sem("resid_made")
        s_st = sem("ln_stats")
        s_ag = sem("ln_aggregated")
        s_sq = sem("ln_std")
        s_rs = sem("ln_rstd")
        s_z = sem("ln_steps")
        s_x1 = sem("x1_made")
        s_wh = sem("wh_filled")
        s_whc = sem("wh_copied")
        s_ab = sem("gat_filled")
        s_gv = sem("gat_vector")
        s_xy = sem("gat_scalar")
        s_cr = sem("c_turned")
        s_cs = sem("c_stored")
        s_cb = [sem(f"c_loaded{i}") for i in range(2)]
        s_pr = sem("products_made")
        s_wh_hi = sem("w_hi_made")
        s_wl = sem("w_lo_made")
        s_vones = sem("v_ones_set")
        s_eb = sem("edge_b_made")
        s_mf = sem("m_filled")
        s_ms = sem("m_sum_made")
        s_m1 = sem("g_made")
        s_o1 = sem("ctx1_filled")
        s_d1 = sem("den1_steps")
        s_c1 = sem("ctx1_scaled")
        s_x1m = sem("x1_less_one")
        s_ee = sem("elu_exp_made")
        s_y = sem("elu_steps")
        s_res = sem("result_made")
        s_out = sem("out_stored")

        s_gate_p = sem("pool_went_on")
        s_gate_v = sem("vector_went_on")
        s_gate_t = sem("tensor_went_on")

        block = ctx.enter_context(nc.Block())

        @block.sync
        def _(sp):
            for s, n in ((s_cl, 2), (s_o0, 4), (s_sc, 4), (s_add, 4), (s_m1, 4), (s_o1, 4),
                         (s_c1, 2), (s_mf, 2), (s_ms, 2)):
                sp.sem_inc(s, n)

            def load_x(b, g):
                xb = x[bass.ds(b, 1), :, :].rearrange("o (t p) f -> p (o t) f", p=P)
                sp.dma_start(x_in[g], xb[:, 4 * g:4 * g + 4, :]).then_inc(s_x[g], 16)

            def keep_x(b):
                sp.dma_start(x_keep[:, :, :],
                             x[bass.ds(b, 1), :, :].rearrange("o (t p) f -> p (o t) f", p=P)).then_inc(s_xk, 16)

            def stack(b, p):
                for t in range(2):
                    tok, chunks = slice(t * HALF, t * HALF + HALF), slice(t * NC // 2, (t + 1) * NC // 2)
                    sp.wait_ge(s_lo, b * 16 + 8 * p + 4 * (t + 1))
                    for e in range(2):
                        h, rows = 2 * p + e, slice(D * e, D * e + D)
                        for k in range(2):
                            half = slice(D * k, D * k + D)
                            sp.dma_start(q16[half, :, h, tok], parts[rows, 0:2, tok]).then_inc(s_stack[p][t], 16)
                            sp.dma_start(k16_v[half, chunks, h, :], parts[rows, 2 + k, tok].rearrange(
                                "p (c n) -> p c n", n=CHUNK)).then_inc(s_stack[p][t], 16)

            def rows_of_c(b, next_x):
                sp.wait_ge(s_cr, b + 1)
                cb = c_dram[bass.ds(b, 1), :, :]
                sp.dma_start(cb.rearrange("o h (t n) -> (o h t) n", t=NT), c_t).then_inc(s_cs, 16)
                sp.wait_ge(s_cs, 16 * b + 16)
                for g in range(GROUPS1):
                    half, h = divmod(g, H)
                    if g >= 2:
                        sp.wait_ge(s_m1, b * UNITS1 + (g - 1) * NT + 4)
                    row = cb[:, h, half * HALF:half * HALF + HALF].rearrange("o n -> (o n)").partition_broadcast(P)
                    sp.dma_start(c_all[:, g % 2, :], row).then_inc(s_cb[g % 2], 16)
                    if g == 1 and next_x:
                        sp.wait_ge(s_wh, (b + 1) * NC)
                        for i in range(NG):
                            load_x(b + 1, i)

            def store(b):
                ob = out[bass.ds(b, 1), :, :].rearrange("o (t p) f -> p (o t) f", p=P)
                for g in range(NG):
                    sp.wait_ge(s_res, b * NG + g + 1)
                    sp.dma_start(ob[:, 4 * g:4 * g + 4, :], x_keep[:, 4 * g:4 * g + 4, :]).then_inc(s_out, 16)

            for k, w in enumerate((Wq, Wk, Wv, Wo)):
                sp.dma_start(w_nat[:, k, :, :], w.rearrange("(t p) f -> p t f", p=P)).then_inc(s_w, 16)
            sp.dma_start(w1[:, :, :], W1.rearrange("(t p) f -> p t f", p=P)).then_inc(s_w, 16)
            sp.dma_start(a_all, a1.rearrange("h (s d) -> h s d", s=2).partition_broadcast(P)).then_inc(s_w, 16)
            for k, v in enumerate((bq, bk, bv)):
                sp.dma_start(b_qk[:, k, :], v.rearrange("(t p) -> p t", p=P),
                             allow_slow_non_contiguous=True).then_inc(s_w, 16)
            for t, v in ((gamma_all, gamma), (beta_all, beta)):
                sp.dma_start(t[:, :], v.partition_broadcast(P)).then_inc(s_w, 16)
            for k, v in enumerate((bo, beta)):
                sp.dma_start(bo_row[0:1, k, :], v.partition_broadcast(1)).then_inc(s_w, 16)
            for g in range(2):
                load_x(0, g)
            keep_x(0)
            for t in range(NT):
                if t >= 2:
                    sp.wait_ge(s_nz, t - 1)
                sp.dma_start(adj_rows[:, t % 2, :], adj[t * P:(t + 1) * P, :]).then_inc(s_adj[t % 2], 16)
            sp.wait_ge(s_nz, NT)
            for g in range(2, NG):
                load_x(0, g)
            for p in range(FT):
                stack(0, p)
            with sp.Fori(0, B - 1) as b:
                rows_of_c(b, True)
                stack(b + 1, 0)
                store(b)
                stack(b + 1, 1)
                sp.wait_ge(s_out, (b + 1) * (16 * NG))
                keep_x(b + 1)
            rows_of_c(B - 1, False)
            store(B - 1)
            sp.wait_ge(s_out, 16 * NG * B)

        @block.gpsimd
        def _(pool):
            nc.gpsimd.memset(ident[:, :], 0.0).then_inc(s_ones, 1)
            nc.gpsimd.memset(ones[:, :], 1.0).then_inc(s_ones, 1)
            nc.gpsimd.memset(consts[:, 0:1], EPS).then_inc(s_ones, 1)
            nc.gpsimd.memset(consts[:, 1:2], SHIFT).then_inc(s_ones, 1)
            nc.gpsimd.memset(consts[:, 2:3], SHIFT0).then_inc(s_ones, 1)
            nc.gpsimd.memset(consts[:, 3:4], -CLIP).then_inc(s_ones, 1)
            pool.wait_ge(s_ones, 6)
            nc.gpsimd.affine_select(out=ident[:, :], in_=ident[:, :], compare_op=ALU.not_equal, fill=1.0,
                                    base=0, pattern=[[-1, P]], channel_multiplier=1).then_inc(s_ones, 1)
            pool.wait_ge(s_ones, 7)
            nc.gpsimd.tensor_copy(ident_b[:, :], ident[:, :]).then_inc(s_const, 1)
            for s in (s_clip_v, s_clip_s):
                pool.wait_ge(s, NT)
            for j in range(NT):
                nc.gpsimd.tensor_scalar(edge[:, j * N:j * N + N], clip_hi[:, j, :], 0.5 / CLIP, 0.5,
                                        ALU.mult, ALU.add).then_inc(s_edge, 1)

            def low0(b, c, n):
                pool.wait_ge(s_e0, b * (NC * UNITS0) + c * UNITS0 + n + 1)
                nc.gpsimd.tensor_tensor(probs0_lo[:, n % 4, :, :], probs0[:, n % 4, :, :],
                                        probs0_hi[:, n % 4, :, :], ALU.subtract).then_inc(s_lo_p, 1)

            def add0(b, c, n):
                h, g = n // NG, n % NG
                pool.wait_ge(s_sc, b * (NC * UNITS0) + c * UNITS0 + n + 5)
                acc = ctxs[:, 4 * g:4 * g + 4, h * D:h * D + D]
                nc.gpsimd.tensor_tensor(acc, acc, scaled[:, n % 4, :, :], ALU.add).then_inc(s_add, 1)

            def chunk0(b, c, first=False, second=False):
                for n in range(UNITS0):
                    if n % 2 == 0:
                        low0(b, c, n)
                    if first:
                        continue
                    if n >= ADD_LAG:
                        add0(b, c, n - ADD_LAG)
                    elif not second:
                        add0(b, c - 1, n - ADD_LAG + UNITS0)

            with pool.Fori(0, B) as b:
                pool.wait_ge(s_c1, b * GROUPS1 + 2)
                pool.sem_inc(s_gate_p, 1)
                nc.gpsimd.memset(v_hi_v[:, :, :, :, D:DV].rearrange("p c h t d -> p (c h t) d"),
                                 1.0).then_inc(s_vones, 1)
                chunk0(b, 0, first=True)
                pool.wait_ge(s_xk, 16 * b + 16)
                pool.wait_ge(s_w, 16 * 13)
                nc.gpsimd.tensor_tensor(x_keep[:, :, :], x_keep[:, :, :],
                                        beta_all[:, :].unsqueeze(1).to_broadcast([P, NT, F]),
                                        ALU.add).then_inc(s_beta, 1)
                chunk0(b, 1, second=True)
                with pool.Fori(2, NC) as c:
                    chunk0(b, c)
                for n in range(UNITS0 - ADD_LAG, UNITS0):
                    add0(b, NC - 1, n)
                nc.gpsimd.memset(v1_v[:, :, :, :, D:DV].rearrange("p c h t d -> p (c h t) d"),
                                 1.0).then_inc(s_vones, 1)
                pool.wait_ge(s_turn, b * 24 + 24)
                pool.sem_inc(s_gate_p, 1)
                nc.gpsimd.tensor_scalar(x_keep[:, :, :], x_keep[:, :, :], 1.0, -1.0,
                                        ALU.mult, ALU.add).then_inc(s_x1m, 1)

        @block.tensor
        def _(pe):
            pe.wait_ge(s_const, 1)
            pe.wait_ge(s_w, 16 * 13)
            for k in range(4):
                for f in range(FT):
                    m = k * FT + f
                    if m >= 4:
                        pe.wait_ge(s_wcopy, m - 3)
                    for t in range(FT):
                        last = nc.tensor.transpose(ps[:, m % 4, t * P:t * P + P],
                                                   w_nat[:, k, t, f * P:f * P + P], ident[:, :])
                    last.then_inc(s_wturn, 1)
            pe.wait_ge(s_wcopy, 4 * FT)
            for f in range(FT):
                last = nc.tensor.matmul(ps[0:1, 4, 0:F], b_qk[:, 2, f:f + 1], w_t[:, 3, f, :],
                                        start=(f == 0), stop=(f == FT - 1))
            last.then_inc(s_bias, 1)
            for t in range(NT):
                pe.wait_ge(s_nz, t + 1)
                for half in range(2):
                    m = 2 * t + half
                    if m >= 4:
                        pe.wait_ge((s_clip_v, s_clip_s)[half], t - 1)
                    bank = ps[:, m % 4, :].bitcast(BF16)
                    for j in range(8):
                        jt = 8 * half + j
                        last = nc.tensor.transpose(bank[:, j * P:j * P + P],
                                                   nz[:, t % 2, jt * P:jt * P + P], ident_b[:, :])
                    last.then_inc(s_adj_t, 1)
            for s in (s_clip_v, s_clip_s):
                pe.wait_ge(s, NT)

            def turn(b, r, groups, src, ready, banks=(0, 1, 2, 3)):
                for g in groups:
                    ready(g)
                    for f in range(FT):
                        i = FT * TURNS[r].index(g) + f
                        if i >= 4:
                            pe.wait_ge(s_turn_c, b * 24 + 8 * r + i - 3)
                        for t in range(4):
                            last = nc.tensor.transpose(ps[:, banks[i % 4], t * P:t * P + P],
                                                       src(4 * g + t)[:, f * P:f * P + P], ident[:, :])
                        last.then_inc(s_turn, 1)

            def turned(b, r, n):
                pe.wait_ge(s_turn_c, b * 24 + 8 * r + FT * n)

            def tokens_by_features(m, bank, w, row=None):
                for t in range(2):
                    o = ps[:, bank, t * F:t * F + F]
                    g, tok = m // 2, slice((2 * (m % 2) + t) * P, (2 * (m % 2) + t + 1) * P)
                    for f in range(FT):
                        last = nc.tensor.matmul(o, x_t[:, g, f, tok], w[:, f, :], start=(f == 0),
                                                stop=(f == FT - 1 and row is None))
                    if row is not None:
                        last = nc.tensor.matmul(o, ones[0:1, :], row, start=False, stop=True)
                return last

            def project_qk(b, p):
                for m in range(2 * NG):
                    g, k = m // 2, m % 2
                    if m >= 4:
                        pe.wait_ge(s_lo, b * 16 + 8 * p + m - 3)
                    for f in range(FT):
                        last = nc.tensor.matmul(ps[:, PREP_BANKS[m % 4], :], w_t[:, k, f, p * P:p * P + P],
                                                x_t[:, g, f, :],
                                                start=(f == 0), stop=(f == FT - 1))
                    last.then_inc(s_qk, 1)

            def scores0(b, c, n):
                h, g = n // NG, n % NG
                pe.wait_ge(s_cl, b * (NC * UNITS0) + c * UNITS0 + n + 1)
                for j in range(2):
                    o = ps[:, 2 * (n % 2) + j, :]
                    keys = k16[:, bass.ds(c * (H * CHUNK) + h * CHUNK + j * P, P)]
                    for k in range(2):
                        last = nc.tensor.matmul(o, keys, q16[:, k, h, g * 512:g * 512 + 512],
                                                start=(k == 0), stop=(k == 1))
                last.then_inc(s_s0, 1)

            def context0(b, c, n):
                h = n // NG
                pe.wait_ge(s_lo_v if n % 2 else s_lo_p, b * (NC * UNITS0 // 2) + c * (UNITS0 // 2) + n // 2 + 1)
                pe.wait_ge(s_sc, b * (NC * UNITS0) + c * UNITS0 + n + 1)
                for j in range(2):
                    v = ((v_hi[:, bass.ds(c * (2 * H * DV) + (2 * h + j) * DV, DV)], DV),
                         (v_lo[:, bass.ds(c * (2 * H * D) + (2 * h + j) * D, D)], D))
                    for t in range(4):
                        for i, part in enumerate((probs0_hi, probs0_lo)):
                            for k, (cols, width) in enumerate(v):
                                last = nc.tensor.matmul(
                                    ps[:, 4 + n % 4, t * DV:t * DV + width],
                                    part[:, n % 4, j, t * P:t * P + P], cols,
                                    start=(j == 0 and t == 0 and i == 0 and k == 0), stop=(j == 1 and i == 1),
                                    skip_group_check=True)
                last.then_inc(s_o0, 1)

            def chunk0(b, c, first):
                for n in range(UNITS0):
                    if first and n == 2 * NG:
                        for t in range(2):
                            pe.wait_ge(s_stack[1][t], (b + 1) * STACKED)
                    scores0(b, c, n)
                    if n >= CTX_LAG:
                        context0(b, c, n - CTX_LAG)
                    elif not first:
                        context0(b, c - 1, n - CTX_LAG + UNITS0)

            def sums1(b, g, q, k, first):
                h = g % H
                pe.wait_ge(s_m1, b * UNITS1 + q * 4 + (g * NT + k + 5))
                cols = bass.ds(q * (4 * H * DX) + (k // 2 * 2 * H + 2 * h + k % 2) * DX, DX)
                for t in range(NT // 2):
                    o = ps[:, 3 * (g % 2) + t // SLOTS, t % SLOTS * DX:(t % SLOTS + 1) * DX]
                    for i, part in enumerate((w_hi, w_lo)):
                        last = nc.tensor.matmul(o, g_bufs[:, k, t * P:t * P + P], part[:, cols],
                                                start=(first and i == 0 and t % SLOTS == 0), stop=False,
                                                skip_group_check=True)
                last.then_inc(s_o1, 1)

            def m_step(b, g, q, u):
                h = g % H
                step = b * M_STEPS + q * 2 + (NT // 2 * g + u)
                pe.wait_ge(s_eb, step + 1)
                pe.wait_ge(s_ms, step + 1)
                for j in range(NT):
                    for part in (w_hi, w_lo):
                        y = part.rearrange("p (c h t d) -> p c t h d", c=NC, h=H, t=2)[:, j // 2, j % 2, h, DV:DX]
                        last = nc.tensor.matmul(ps[:, 6 + u, 0:DV], edge_b[:, u, j, :], y,
                                                start=(j == 0 and part is w_hi), stop=(j == NT - 1 and part is w_lo))
                last.then_inc(s_mf, 1)

            def quad1(b, g, q, first):
                for k in range(4):
                    sums1(b, g, q, k, first and k == 0)
                    if k % 2 == 1:
                        m_step(b, g, q, k // 2)

            def prepare(b):
                pe.wait_ge(s_c1, b * GROUPS1 + 1)
                pe.wait_ge(s_ms, b * M_STEPS + 1)
                turn(b, 0, TURNS[0], lambda t: x_in[t // 4][:, t % 4, :],
                     lambda g: pe.wait_ge(s_x[g], 16 * b + 16), PREP_BANKS)
                turned(b, 0, NG)
                for m in range(NC):
                    if m >= 4:
                        pe.wait_ge(s_vc, b * NC + m - 3)
                    tokens_by_features(m, PREP_BANKS[m % 4], w_t[:, 2, :, :]).then_inc(s_v, 1)
                pe.wait_ge(s_vc, b * NC + NC)
                project_qk(b, 0)
                pe.wait_ge(s_lo, b * 16 + 8)
                project_qk(b, 1)
                pe.wait_ge(s_lo, b * 16 + 16)

            def layers(b):
                pe.wait_ge(s_vones, 2 * b + 1)
                for t in range(2):
                    pe.wait_ge(s_stack[0][t], (b + 1) * STACKED)
                chunk0(b, 0, True)
                with pe.Fori(1, NC) as c:
                    chunk0(b, c, False)
                for n in range(UNITS0 - CTX_LAG, UNITS0):
                    context0(b, NC - 1, n)
                turn(b, 1, TURNS[1], lambda t: ctxs[:, t, :],
                     lambda g: pe.wait_ge(s_add, (b + 1) * ((NC - 1) * UNITS0) + g + 1))
                for m in range(NC):
                    if m % 2 == 0:
                        turned(b, 1, m // 2 + 1)
                    if m >= 4:
                        pe.wait_ge(s_r, b * NC + m - 3)
                    tokens_by_features(m, 4 + m % 4, w_t[:, 3, :, :], bias_row[0:1, :]).then_inc(s_wo, 1)
                turn(b, 2, TURNS[2], lambda t: x_keep[:, t, :], lambda g: pe.wait_ge(s_x1, b * NG + g + 1))
                for t in range(NT):
                    if t % 4 == 0:
                        turned(b, 2, t // 4 + 1)
                    for f in range(FT):
                        last = nc.tensor.matmul(ps[:, 7, t * 2 * H:(t + 1) * 2 * H],
                                                x_t[:, t // 4, f, t % 4 * P:t % 4 * P + P],
                                                wa[:, f, :, :], start=(f == 0), stop=(f == FT - 1))
                last.then_inc(s_ab, 1)
                pe.wait_ge(s_gv, b * 7 + 1)
                nc.tensor.transpose(ps[0:H, 6, 0:P], gat_max[:, :], ident[:, :]).then_inc(s_ab, 1)
                pe.wait_ge(s_gv, b * 7 + 3)
                nc.tensor.matmul(ps[:, 6, 256:256 + H], ones[0:H, :], gat_diag[:, :],
                                 start=True, stop=True).then_inc(s_ab, 1)
                for m in range(NC):
                    if m == 1:
                        pe.wait_ge(s_gv, b * 7 + 6)
                        pe.sem_inc(s_gate_t, 1)
                        nc.tensor.transpose(ps[0:H * NT, 6, 384:384 + P],
                                            gat_c[:, :, :].rearrange("p h t -> p (h t)"),
                                            ident[:, :]).then_inc(s_ab, 1)
                    if m >= 2:
                        pe.wait_ge(s_whc, b * NC + m - 1)
                    tokens_by_features(m, 4 + m % 2, w1).then_inc(s_wh, 1)
                pe.wait_ge(s_wl, b * NC + NC)
                for g in range(GROUPS1):
                    pe.wait_ge(s_c1, b * GROUPS1 + g + 1)
                    quad1(b, g, 0, True)
                    with pe.Fori(1, NT // 4) as q:
                        quad1(b, g, q, False)

            prepare(0)
            with pe.Fori(0, B - 1) as b:
                layers(b)
                prepare(b + 1)
            layers(B - 1)

        @block.scalar
        def _(act):
            def turn(b, r, groups):
                for g in groups:
                    i = TURNS[r].index(g)
                    for f in range(FT):
                        act.wait_ge(s_turn, b * 24 + 8 * r + FT * i + (FT if r == 0 else f + 1))
                        bank = (PREP_BANKS if r == 0 else range(4))[(FT * i + f) % 4]
                        nc.scalar.activation(x_t[:, g, f, :], ps[:, bank, :], ACT.Copy).then_inc(s_turn_c, 1)

            def high_parts(b, p):
                for m in range(2 * NG):
                    g, k = m // 2, m % 2
                    act.wait_ge(s_qk, b * 16 + 8 * p + m + 1)
                    if p == 1 and m % 4 == 0:
                        act.wait_ge(s_stack[0][m // 4], (b + 1) * STACKED)
                    nc.scalar.activation(parts[:, 2 * k, g * 512:g * 512 + 512], ps[:, PREP_BANKS[m % 4], :],
                                         ACT.Identity,
                                         bias=b_qk[:, k, p:p + 1]).then_inc(s_hi, 1)

            def exp0(b, c, n):
                act.wait_ge(s_cl, b * (NC * UNITS0) + c * UNITS0 + n + 3)
                nc.scalar.activation(probs0[:, n % 4, :, :], probs0[:, n % 4, :, :], ACT.Exp,
                                     scale=0.125, bias=consts[:, 2:3]).then_inc(s_e0, 1)

            def scale0(b, c, n, first=False):
                h, g = n // NG, n % NG
                act.wait_ge(s_rd, b * (NC * UNITS0) + c * UNITS0 + n + 1)
                if not first:
                    act.wait_ge(s_add, b * ((NC - 1) * UNITS0) + (c - 1) * UNITS0 + n + 1)
                for t in range(4):
                    dst = ctxs[:, 4 * g + t, h * D:h * D + D] if first else scaled[:, n % 4, t, :]
                    last = nc.scalar.activation(dst, ps[:, 4 + n % 4, t * DV:t * DV + D],
                                                ACT.Copy, scale=rden[:, n % 4, t:t + 1])
                last.then_inc(s_sc, 1)

            def chunk0(b, c, first=False, second=False):
                for n in range(UNITS0):
                    exp0(b, c, n)
                    if first and n == DEN_LAG:
                        for t in range(2):
                            act.wait_ge(s_stack[1][t], (b + 1) * STACKED)
                    if n >= DEN_LAG:
                        scale0(b, c, n - DEN_LAG, first)
                    elif not first:
                        scale0(b, c - 1, n - DEN_LAG + UNITS0, second)

            def edges_b(b, g, p, u):
                act.wait_ge(s_mf, b * M_STEPS + p * 2 + (NT // 2 * g + u + 1))
                nc.scalar.activation(edge_b[:, u, :, :],
                                     edge[:, :].rearrange("p (j n) -> p j n", j=NT)[
                                         :, :, bass.ds(p * (2 * P) + (u * P + g // H * HALF), P)],
                                     ACT.Copy).then_inc(s_eb, 1)

            def m_copy(b, g, p, u):
                act.wait_ge(s_mf, b * M_STEPS + p * 2 + (NT // 2 * g + u + 3))
                to = ((g // H * NT // 2 + u) * H + g % H) * DV
                nc.scalar.activation(v1[:, bass.ds(p * (2 * H * DV) + to, DV)], ps[:, 6 + u, 0:DV],
                                     ACT.Copy).then_inc(s_ms, 1)

            def root(b, i, tiles):
                act.wait_ge(s_ag, b * 5 + i)
                nc.scalar.activation(std[:, tiles], mv[:, tiles, 1], ACT.Sqrt, bias=consts[:, 0:1]).then_inc(s_sq, 1)

            def elu_exp(b, g):
                if g >= 2:
                    act.wait_ge(s_y, b * 2 * NG + 2 * (g - 2) + 2)
                nc.scalar.activation(elu_e[:, g % 2, :, :], ctxs[:, 4 * g:4 * g + 4, :],
                                     ACT.Exp).then_inc(s_ee, 1)

            def v_high(b, m):
                act.wait_ge(s_v, b * NC + m + 1)
                nc.scalar.activation(v_hi_v[:, m, :, :, 0:D],
                                     ps[:, PREP_BANKS[m % 4], :].rearrange("p (t h d) -> p h t d", t=2, h=H),
                                     ACT.Copy).then_inc(s_vh, 1)

            def between(b, tail, prepare):
                if prepare:
                    turn(b + 1, 0, TURNS[0])
                if tail:
                    act.wait_ge(s_c1, b * GROUPS1 + GROUPS1 + 2)
                    elu_exp(b, 0)
                for g in range(NG):
                    if tail and g + 1 < NG:
                        elu_exp(b, g + 1)
                    if prepare:
                        v_high(b + 1, 2 * g)
                        v_high(b + 1, 2 * g + 1)
                if prepare:
                    act.wait_ge(s_w, 16 * 13)
                    if tail:
                        act.wait_ge(s_y, (b + 1) * (2 * NG))
                    high_parts(b + 1, 0)
                if tail:
                    root(b, 5, slice(0, NT))
                if prepare:
                    high_parts(b + 1, 1)

            def layers(b):
                chunk0(b, 0, first=True)
                chunk0(b, 1, second=True)
                with act.Fori(2, NC) as c:
                    chunk0(b, c)
                for n in range(UNITS0 - DEN_LAG, UNITS0):
                    scale0(b, NC - 1, n)
                turn(b, 1, TURNS[1])
                for i in range(4):
                    root(b, i + 1, slice(NT // 2 * (i % 2), NT // 2 * (i % 2 + 1)))

                def wh_copy(m):
                    act.wait_ge(s_wh, b * NC + m + 1)
                    nc.scalar.activation(v1_v[:, m, :, :, 0:D],
                                         ps[:, 4 + m % 2, :].rearrange("p (t h d) -> p h t d", t=2, h=H),
                                         ACT.Copy).then_inc(s_whc, 1)

                turn(b, 2, TURNS[2])
                wh_copy(0)
                act.wait_ge(s_ab, b * 4 + 4)
                nc.scalar.activation(c_t, ps[0:H * NT, 6, 384:384 + P], ACT.Copy).then_inc(s_cr, 1)
                act.wait_ge(s_gv, b * 7 + 6)
                nc.scalar.activation(gat_x[:, :, :, :], gat_nd[:, :, :, :], ACT.Exp, scale=-1.0,
                                     bias=consts[:, 1:2]).then_inc(s_xy, 1)
                nc.scalar.activation(gat_y[:, :, :, :], gat_nd[:, :, :, :], ACT.Exp, scale=-0.2,
                                     bias=consts[:, 1:2]).then_inc(s_xy, 1)
                nc.scalar.activation(gat_c[:, :, :], gat_c[:, :, :], ACT.Exp, scale=-0.8).then_inc(s_xy, 1)

                def w_high(c):
                    act.wait_ge(s_pr, b * 2 * NC + 2 * c + 2)
                    nc.scalar.activation(w_hi[:, c * (2 * H * DX):(c + 1) * (2 * H * DX)],
                                         prods[:, c % 3, :, :].rearrange("p g d -> p (g d)"),
                                         ACT.Copy).then_inc(s_wh_hi, 1)

                for m in range(1, NC):
                    wh_copy(m)
                    if m >= 2:
                        w_high(m - 2)
                for c in range(NC - 2, NC):
                    w_high(c)
                act.wait_ge(s_edge, NT)
                for u in range(2):
                    edges_b(b, 0, 0, u)
                for g in range(GROUPS1):
                    with act.Fori(0, NT // 4 - 1) as p:
                        for u in range(2):
                            m_copy(b, g, p, u)
                            edges_b(b, g, p + 1, u)
                    for u in range(2):
                        m_copy(b, g, NT // 4 - 1, u)
                        if g + 1 < GROUPS1:
                            edges_b(b, g + 1, 0, u)

            act.wait_ge(s_const, 1)
            for t in range(NT):
                act.wait_ge(s_adj_t, 2 * t + 2)
                nc.scalar.activation(clip_hi[:, 8:16, t * P:t * P + P],
                                     ps[:, (2 * t + 1) % 4, :].bitcast(BF16).rearrange("p (j n) -> p j n", j=8),
                                     ACT.Identity, scale=2 * CLIP, bias=consts[:, 3:4]).then_inc(s_clip_s, 1)
            between(-1, False, True)
            with act.Fori(0, B - 1) as b:
                layers(b)
                between(b, True, True)
            layers(B - 1)
            between(B - 1, True, False)

        @block.vector
        def _(dve):
            dve.wait_ge(s_w, 16 * 13)
            for f in range(FT):
                for s in range(2):
                    nc.vector.tensor_tensor(wa_prod[:, f, s, :, :], w1[:, f, :].rearrange("p (h d) -> p h d", h=H),
                                            a_all[:, :, s, :], ALU.mult).then_inc(s_setup, 1)
            nc.vector.tensor_tensor(bias_row[:, :], bo_row[:, 0, :], bo_row[:, 1, :],
                                    ALU.subtract).then_inc(s_setup, 1)
            dve.wait_ge(s_setup, 5)
            for f in range(FT):
                for s in range(2):
                    nc.vector.tensor_reduce(wa[:, f, s, :], wa_prod[:, f, s, :, :], AX.X, ALU.add).then_inc(s_setup, 1)
            for m in range(4 * FT):
                dve.wait_ge(s_wturn, m + 1)
                nc.vector.tensor_copy(w_t[:, m // FT, m % FT, :], ps[:, m % 4, 0:F]).then_inc(s_wcopy, 1)
            dve.wait_ge(s_bias, 1)
            nc.vector.scalar_tensor_tensor(out=bias_row[:, :], in0=ps[0:1, 4, 0:F], scalar=float(NC),
                                           in1=bias_row[:, :], op0=ALU.mult, op1=ALU.add).then_inc(s_setup, 1)
            def marks(t):
                dve.wait_ge(s_adj[t % 2], 16 * (t // 2) + 16)
                if t >= 2:
                    dve.wait_ge(s_adj_t, 2 * (t - 1))
                nc.vector.tensor_scalar(nz[:, t % 2, :], adj_rows[:, t % 2, :], 0.0, None,
                                        ALU.not_equal).then_inc(s_nz, 1)

            marks(0)
            for t in range(NT):
                if t + 1 < NT:
                    marks(t + 1)
                dve.wait_ge(s_adj_t, 2 * t + 1)
                nc.vector.tensor_scalar(clip_hi[:, 0:8, t * P:t * P + P],
                                        ps[:, 2 * t % 4, :].bitcast(BF16).rearrange("p (j n) -> p j n", j=8),
                                        2 * CLIP, -CLIP, ALU.mult, ALU.add).then_inc(s_clip_v, 1)
            for s in (s_clip_v, s_clip_s):
                dve.wait_ge(s, NT)
            dve.wait_ge(s_setup, 10)

            def low_part(b, p, m):
                g, k = m // 2, m % 2
                dve.wait_ge(s_hi, b * 16 + 8 * p + m + 1)
                tok = slice(g * 512, g * 512 + 512)
                nc.vector.scalar_tensor_tensor(out=parts[:, 2 * k + 1, tok], in0=ps[:, PREP_BANKS[m % 4], :],
                                               scalar=b_qk[:, k, p:p + 1], in1=parts[:, 2 * k, tok],
                                               op0=ALU.add, op1=ALU.subtract).then_inc(s_lo, 1)

            def v_low(b, m):
                dve.wait_ge(s_vh, b * NC + m + 1)
                nc.vector.tensor_tensor(v_lo_v[:, m, :, :, :],
                                        ps[:, PREP_BANKS[m % 4], :].rearrange("p (t h d) -> p h t d", t=2, h=H),
                                        v_hi_v[:, m, :, :, 0:D], ALU.subtract).then_inc(s_vc, 1)

            def clip0(b, c, n):
                h, g = n // NG, n % NG
                unit = b * (NC * UNITS0) + c * UNITS0 + n
                dve.wait_ge(s_s0, unit + 1)
                dve.wait_ge(s_o0, unit + 1)
                nc.vector.scalar_tensor_tensor(out=probs0[:, n % 4, :, :],
                                               in0=ps[:, 2 * (n % 2):2 * (n % 2) + 2, :], scalar=-CLIP,
                                               in1=clip_hi[:, bass.ds(2 * c, 2), g * 512:g * 512 + 512],
                                               op0=ALU.max, op1=ALU.min).then_inc(s_cl, 1)

            def low0(b, c, n):
                dve.wait_ge(s_e0, b * (NC * UNITS0) + c * UNITS0 + n + 1)
                nc.vector.tensor_tensor(probs0_lo[:, n % 4, :, :], probs0[:, n % 4, :, :],
                                        probs0_hi[:, n % 4, :, :], ALU.subtract).then_inc(s_lo_v, 1)

            def invert0(b, c, n):
                unit = b * (NC * UNITS0) + c * UNITS0 + n
                dve.wait_ge(s_o0, unit + 5)
                dve.wait_ge(s_sc, unit + 1)
                nc.vector.reciprocal(rden[:, n % 4, :], ps[:, 4 + n % 4, D:4 * DV:DV]).then_inc(s_rd, 1)

            def chunk0(b, c, first):
                for n in range(UNITS0):
                    clip0(b, c, n)
                    if n >= DEN_LAG:
                        invert0(b, c, n - DEN_LAG)
                    elif not first:
                        invert0(b, c - 1, n - DEN_LAG + UNITS0)
                    if n % 2 == 0 and n >= 1:
                        low0(b, c, n - 1)
                    elif n == 0 and not first:
                        low0(b, c - 1, UNITS0 - 1)

            def stats_of(t, src):
                nc.vector.bn_stats(stats[:, t, :], src[:, t, :]).then_inc(s_st, 1)

            def means(b, made, tiles):
                dve.wait_ge(s_st, b * 3 * NT + made)
                dve.sem_inc(s_gate_v, 1)
                for t in tiles:
                    last = nc.vector.bn_aggr(mv[:, t, :], stats[:, t, :])
                last.then_inc(s_ag, 1)

            def inverse_root(b, i, tiles):
                dve.wait_ge(s_sq, b * 5 + i)
                nc.vector.reciprocal(rstd[:, tiles], std[:, tiles]).then_inc(s_rs, 1)
                dve.wait_ge(s_rs, b * 5 + i)

            def normalise(t, dst, src):
                return nc.vector.tensor_scalar(dst[:, t, :], src[:, t, :], mv[:, t, 0:1], rstd[:, t:t + 1],
                                               ALU.subtract, ALU.mult)

            def mask1(b, g, q, k):
                half, h = divmod(g, H)
                dve.wait_ge(s_o1, b * UNITS1 + q * 4 + (g * NT + k + 1))
                nd = gat_nd[:, :, :, :].rearrange("p c h t -> p (c h t)")
                nc.vector.scalar_tensor_tensor(out=g_bufs[:, k, :],
                                               in0=c_all[:, g % 2, :],
                                               scalar=nd[:, bass.ds(q * (4 * H) + (k // 2 * 2 * H + 2 * h + k % 2), 1)],
                                               in1=edge[:, bass.ds(q * (4 * N) + (k * N + half * HALF), HALF)],
                                               op0=ALU.is_gt, op1=ALU.mult).then_inc(s_m1, 1)

            def scale1(b, g):
                half, h = divmod(g, H)
                tiles = slice(half * NT // 2, (half + 1) * NT // 2)
                o = ps[:, 3 * (g % 2):3 * (g % 2) + 3, 0:SLOTS * DX].rearrange("p k (s d) -> p k s d", d=DX)
                pieces = ((0, 2, SLOTS), (2, 3, NT // 2 - 2 * SLOTS))
                dve.wait_ge(s_o1, b * UNITS1 + (g + 1) * NT + 4)
                dve.wait_ge(s_ms, b * M_STEPS + (NT // 2 * (g + 1) + 2))
                step = b * 7 * GROUPS1 + 7 * g
                for k0, k1, ns in pieces:
                    t0 = k0 * SLOTS
                    piece = slice(t0, t0 + (k1 - k0) * ns)
                    m = m_sum[:, half * NT // 2 + t0:half * NT // 2 + t0 + (k1 - k0) * ns, h, :]
                    nc.vector.tensor_tensor(gat_s[:, piece, :].rearrange("p (k s) d -> p k s d", s=ns),
                                            m.rearrange("p (k s) d -> p k s d", s=ns), o[:, k0:k1, 0:ns, DV:DX],
                                            ALU.subtract).then_inc(s_d1, 1)
                dve.wait_ge(s_d1, step + 2)
                nc.vector.tensor_tensor(gat_s[:, :, :], gat_s[:, :, :],
                                        gat_c[:, h, tiles].unsqueeze(2).to_broadcast([P, NT // 2, DV]),
                                        ALU.mult).then_inc(s_d1, 1)
                dve.wait_ge(s_d1, step + 3)
                for k0, k1, ns in pieces:
                    t0 = k0 * SLOTS
                    gs = gat_s[:, t0:t0 + (k1 - k0) * ns, :].rearrange("p (k s) d -> p k s d", s=ns)
                    nc.vector.tensor_tensor(gs, o[:, k0:k1, 0:ns, 0:DV], gs, ALU.add).then_inc(s_d1, 1)
                dve.wait_ge(s_d1, step + 5)
                nc.vector.tensor_scalar(gat_den[:, :], gat_s[:, :, D], 1e-37, None, ALU.max).then_inc(s_d1, 1)
                dve.wait_ge(s_d1, step + 6)
                nc.vector.reciprocal(gat_rden[:, :], gat_den[:, :]).then_inc(s_d1, 1)
                dve.wait_ge(s_d1, step + 7)
                nc.vector.tensor_tensor(ctxs[:, tiles, h * D:h * D + D], gat_s[:, :, 0:D],
                                        gat_rden[:, :].unsqueeze(2).to_broadcast([P, NT // 2, D]),
                                        ALU.mult).then_inc(s_c1, 1)

            def between(b, tail, prepare):
                if tail:
                    dve.wait_ge(s_x1m, b + 1)
                for g in range(NG):
                    if tail:
                        dve.wait_ge(s_ee, b * NG + g + 1)
                        s4 = slice(4 * g, 4 * g + 4)
                        nc.vector.scalar_tensor_tensor(out=elu_e[:, g % 2, :, :], in0=elu_e[:, g % 2, :, :], scalar=1.0,
                                                       in1=x_keep[:, s4, :], op0=ALU.min, op1=ALU.add).then_inc(s_y, 1)
                        dve.wait_ge(s_y, b * 2 * NG + 2 * g + 1)
                        nc.vector.scalar_tensor_tensor(out=x_keep[:, s4, :], in0=ctxs[:, s4, :], scalar=0.0,
                                                       in1=elu_e[:, g % 2, :, :], op0=ALU.max,
                                                       op1=ALU.add).then_inc(s_y, 1)
                    if prepare:
                        v_low(b + 1, 2 * g)
                        v_low(b + 1, 2 * g + 1)
                for g in range(NG):
                    if tail:
                        dve.wait_ge(s_y, b * 2 * NG + 2 * g + 2)
                        dve.sem_inc(s_gate_v, 1)
                        for t in range(4 * g, 4 * g + 4):
                            stats_of(t, x_keep)
                    if prepare:
                        low_part(b + 1, 0, 2 * g)
                        low_part(b + 1, 0, 2 * g + 1)
                if tail:
                    means(b, 3 * NT, range(NT))
                    inverse_root(b, 5, slice(0, NT))
                for g in range(NG):
                    if tail:
                        for t in range(4 * g, 4 * g + 4):
                            last = normalise(t, x_keep, x_keep)
                        last.then_inc(s_res, 1)
                    if prepare:
                        low_part(b + 1, 1, 2 * g)
                        low_part(b + 1, 1, 2 * g + 1)

            def layers(b):
                chunk0(b, 0, True)
                with dve.Fori(1, NC) as c:
                    chunk0(b, c, False)
                low0(b, NC - 1, UNITS0 - 1)
                for n in range(UNITS0 - DEN_LAG, UNITS0):
                    invert0(b, NC - 1, n)
                halves = (range(0, NT // 2), range(NT // 2, NT))
                dve.wait_ge(s_beta, b + 1)
                for s, tiles in enumerate(halves):
                    for m in range(4 * s, 4 * s + 4):
                        dve.wait_ge(s_wo, b * NC + m + 1)
                        nc.vector.tensor_tensor(ctxs[:, 2 * m:2 * m + 2, :],
                                                ps[:, 4 + m % 4, :].rearrange("p (t f) -> p t f", t=2),
                                                x_keep[:, 2 * m:2 * m + 2, :], ALU.add).then_inc(s_r, 1)
                    for t in tiles:
                        dve.wait_ge(s_r, b * NC + t // 2 + 1)
                        stats_of(t, ctxs)
                    means(b, NT // 2 * (s + 1), tiles)
                for s, tiles in enumerate(halves):
                    made = b * 2 * NT + NT * s
                    inverse_root(b, 1 + s, slice(tiles[0], tiles[-1] + 1))
                    for t in tiles:
                        nc.vector.scalar_tensor_tensor(out=ctxs[:, t, :], in0=ctxs[:, t, :], scalar=mv[:, t, 0:1],
                                                       in1=gamma_all[:, :], op0=ALU.subtract,
                                                       op1=ALU.mult).then_inc(s_z, 1)
                    for i, t in enumerate(tiles):
                        dve.wait_ge(s_z, made + i + 1)
                        nc.vector.scalar_tensor_tensor(out=ctxs[:, t, :], in0=ctxs[:, t, :], scalar=rstd[:, t:t + 1],
                                                       in1=x_keep[:, t, :], op0=ALU.mult, op1=ALU.add).then_inc(s_z, 1)
                    for i, t in enumerate(tiles):
                        dve.wait_ge(s_z, made + NT // 2 + i + 1)
                        stats_of(t, ctxs)
                    means(b, NT + NT // 2 * (s + 1), tiles)
                for s, tiles in enumerate(halves):
                    inverse_root(b, 3 + s, slice(tiles[0], tiles[-1] + 1))
                    for t in tiles:
                        last = normalise(t, x_keep, ctxs)
                        if t % 4 == 3:
                            last.then_inc(s_x1, 1)
                dve.wait_ge(s_ab, b * 4 + 1)
                ab = ps[:, 7, 0:NT * 2 * H]
                nc.vector.tensor_reduce(gat_max[:, :], ab.rearrange("p (t s h) -> p s h t", s=2, h=H)[:, 1, :, :],
                                        AX.X, ALU.max).then_inc(s_gv, 1)
                dve.wait_ge(s_ab, b * 4 + 2)
                nc.vector.tensor_reduce(gat_max4[:, :], ps[0:H, 6, 0:P], AX.X, ALU.max).then_inc(s_gv, 1)
                dve.wait_ge(s_gv, b * 7 + 2)
                nc.vector.tensor_scalar(gat_diag[:, :], ident[0:H, 0:H], gat_max4[:, 0:1], None,
                                        ALU.mult).then_inc(s_gv, 1)
                dve.wait_ge(s_ab, b * 4 + 3)
                nc.vector.tensor_copy(gat_b[:, :], ps[:, 6, 256:256 + H]).then_inc(s_gv, 1)
                dve.wait_ge(s_gv, b * 7 + 4)
                b_cht = ab.rearrange("p (c t s h) -> p s c h t", c=NC, t=2, s=2)[:, 1, :, :, :]
                nc.vector.tensor_tensor(gat_nd[:, :, :, :],
                                        gat_b[:, :].unsqueeze(1).unsqueeze(3).to_broadcast([P, NC, H, 2]), b_cht,
                                        ALU.subtract).then_inc(s_gv, 1)
                nc.vector.tensor_tensor(gat_c[:, :, :], ab.rearrange("p (t s h) -> p s h t", s=2, h=H)[:, 0, :, :],
                                        gat_b[:, :].unsqueeze(2).to_broadcast([P, H, NT]), ALU.add).then_inc(s_gv, 1)
                dve.wait_ge(s_xy, b * 3 + 3)
                nc.vector.tensor_scalar(gat_c[:, :, :], gat_c[:, :, :], 1.0, None, ALU.min).then_inc(s_gv, 1)

                dve.wait_ge(s_vones, 2 * b + 2)

                def products(c):
                    dve.wait_ge(s_whc, b * NC + c + 1)
                    if c >= 3:
                        dve.wait_ge(s_wl, b * NC + c - 2)
                    w = v1[:, :].rearrange("p (g d) -> p g d", d=DV)[:, 2 * H * c:2 * H * (c + 1), :]
                    for i, f in enumerate((gat_x, gat_y)):
                        nc.vector.tensor_tensor(prods[:, c % 3, :, i * DV:(i + 1) * DV], w,
                                                f[:, c, :, :].rearrange("p h t -> p (h t)").unsqueeze(2)
                                                .to_broadcast([P, 2 * H, DV]), ALU.mult).then_inc(s_pr, 1)

                def low_of_products(c):
                    dve.wait_ge(s_wh_hi, b * NC + c + 1)
                    cols = slice(c * (2 * H * DX), (c + 1) * (2 * H * DX))
                    nc.vector.tensor_tensor(w_lo[:, cols], prods[:, c % 3, :, :].rearrange("p g d -> p (g d)"),
                                            w_hi[:, cols], ALU.subtract).then_inc(s_wl, 1)

                for c in range(NC):
                    products(c)
                    if c >= 2:
                        low_of_products(c - 2)
                low_of_products(NC - 2)
                low_of_products(NC - 1)
                for g in range(GROUPS1):
                    dve.wait_ge(s_cb[g % 2], 64 * b + 16 * (g // 2) + 16)
                    for k in range(4):
                        mask1(b, g, 0, k)
                    if g >= 1:
                        scale1(b, g - 1)
                    with dve.Fori(1, NT // 4) as q:
                        for k in range(4):
                            mask1(b, g, q, k)
                scale1(b, GROUPS1 - 1)

            between(-1, False, True)
            with dve.Fori(0, B - 1) as b:
                layers(b)
                between(b, True, True)
            layers(B - 1)
            between(B - 1, True, False)


_INS = ['x', 'adj', 'L0_gnn_Wq', 'L0_gnn_bq', 'L0_gnn_Wk', 'L0_gnn_bk', 'L0_gnn_Wv', 'L0_gnn_bv', 'L0_gnn_Wo',
        'L0_gnn_bo', 'L0_gnn_gamma', 'L0_gnn_beta', 'L1_gnn_W', 'L1_gnn_a']


def kernel(**inputs):
    import numpy as _np
    import concourse.bacc as _bacc
    from concourse import mybir as _mybir
    from concourse.bass_utils import run_bass_kernel_spmd as _run

    nc = _bacc.Bacc("TRN2", target_bir_lowering=False, num_devices=1)
    arrays, args = {}, []
    for name in _INS:
        a = _np.ascontiguousarray(inputs[name])
        arrays[f"in_{name}_dram"] = a
        args.append(nc.dram_tensor(f"in_{name}_dram", a.shape, _mybir.dt.from_np(a.dtype), kind="ExternalInput").ap())
    args.append(nc.dram_tensor("out_0_dram", (B, N, F), F32, kind="ExternalOutput").ap())
    build(nc, *args)
    r = _run(nc, [arrays], core_ids=[0])
    return r.results[0]["out_0_dram"]
```
